# Optimizing a Trainium2 kernel written in Bass

```python
import numpy as np
import jax
import jax.numpy as jnp

def _softmax(x, axis=-1):
    return jax.nn.softmax(x, axis=axis)
def _gelu(x):
    return jax.nn.gelu(x, approximate=True)
def _silu(x):
    return jax.nn.silu(x)
def _sigmoid(x):
    return jax.nn.sigmoid(x)
def _layernorm(x, axis=-1, eps=1e-5):
    m = jnp.mean(x, axis=axis, keepdims=True)
    v = jnp.var(x, axis=axis, keepdims=True)
    return (x - m) / jnp.sqrt(v + eps)
def _scatter_add(tgt, idx, src, axis=0):
    return tgt.at[idx].add(src)
def _segment_sum(src, seg, n):
    return jax.ops.segment_sum(src, seg, n)

kernel_name = 'mk_conv_preact_d4_conv_nchw32_f9a659'

def setup_inputs(seed: int = 0):
    np.random.seed(seed)
    _w = jnp.asarray
    def _rec_inputs():
        import jax
        import jax.numpy as jnp
        _gk = jax.random.key(seed)
        x = -7.109e-05 + 0.9999 * jax.random.normal(jax.random.fold_in(_gk, 1), (16, 32, 256, 256), jnp.float32)
        return x
    x = _rec_inputs()
    def _L0_conv_setup():
        import jax, jax.numpy as jnp
        import numpy as np
        from jax import lax
        C_IN, C_OUT, K = (32, 32, 3)
        DIV = float(np.sqrt(C_IN * K * K))
        key = jax.random.key(seed)
        kx, kw = jax.random.split(key)
        x = jax.random.normal(kx, (32, C_IN, 256, 256), dtype=jnp.float32)
        weight = 0.01 * jax.random.normal(kw, (C_OUT, C_IN, K, K), dtype=jnp.float32)
        return {'x': x, 'weight': weight}
    _L0_conv_all = _L0_conv_setup()
    _L0_conv_in = {k: v for k, v in _L0_conv_all.items() if k in ('weight', )}
    del _L0_conv_all

    def _L1_conv_setup():
        import jax, jax.numpy as jnp
        import numpy as np
        B, C_IN, C_OUT, H, W, M1, M2 = (16, 32, 32, 256, 256, 16, 16)
        key = jax.random.key(seed)
        k1, k2, k3 = jax.random.split(key, 3)
        scale = 1.0 / (C_IN * C_OUT)
        x = jax.random.normal(k1, (B, C_IN, H, W), dtype=jnp.float32)
        weights1 = scale * jax.random.normal(k2, (C_IN, C_OUT, M1, M2, 2), dtype=jnp.float32)
        weights2 = scale * jax.random.normal(k3, (C_IN, C_OUT, M1, M2, 2), dtype=jnp.float32)
        return {'x': x, 'weights1': weights1, 'weights2': weights2}
    _L1_conv_all = _L1_conv_setup()
    _L1_conv_in = {k: v for k, v in _L1_conv_all.items() if k in ('weights1', 'weights2', )}
    del _L1_conv_all

    def _L2_conv_setup():
        import jax, jax.numpy as jnp
        import numpy as np
        from jax import lax
        B, C, H, W = (16, 32, 384, 384)
        NK = 32
        K = 3
        HID = 128
        key = jax.random.key(seed)
        ks = jax.random.split(key, 5)
        x = jax.random.normal(ks[0], (B, C, H, W), dtype=jnp.float32)
        w1 = jax.random.normal(ks[1], (C, HID), dtype=jnp.float32) * (1.0 / np.sqrt(C))
        b1 = jnp.zeros((HID,), dtype=jnp.float32)
        w2 = jax.random.normal(ks[2], (HID, NK * K * K), dtype=jnp.float32) * (1.0 / np.sqrt(HID))
        b2 = jnp.zeros((NK * K * K,), dtype=jnp.float32)
        return {'x': x, 'w1': w1, 'b1': b1, 'w2': w2, 'b2': b2}
    _L2_conv_all = _L2_conv_setup()
    _L2_conv_in = {k: v for k, v in _L2_conv_all.items() if k in ('w1', 'b1', 'w2', 'b2', )}
    del _L2_conv_all

    def _L3_conv_setup():
        import jax, jax.numpy as jnp
        import numpy as np
        BATCH, IN_DIM, H, W = (16, 32, 128, 128)
        BASE_OUT = 32
        key = jax.random.key(seed)
        k_x, k_w2, k_b2, k_w1, k_b1 = jax.random.split(key, 5)
        x = jax.random.normal(k_x, (BATCH, IN_DIM, H, W), dtype=jnp.float32)
        s2 = 1.0 / np.sqrt(IN_DIM)
        W2 = jax.random.uniform(k_w2, (4 * BASE_OUT, IN_DIM), jnp.float32, -s2, s2)
        b2 = jax.random.uniform(k_b2, (4 * BASE_OUT,), jnp.float32, -s2, s2)
        s1 = 1.0 / np.sqrt(BASE_OUT * 2)
        W1 = jax.random.uniform(k_w1, (4 * BASE_OUT, BASE_OUT, 2), jnp.float32, -s1, s1)
        b1 = jax.random.uniform(k_b1, (4 * BASE_OUT,), jnp.float32, -s1, s1)
        return {'x': x, 'W2': W2, 'b2': b2, 'W1': W1, 'b1': b1}
    _L3_conv_all = _L3_conv_setup()
    _L3_conv_in = {k: v for k, v in _L3_conv_all.items() if k in ('W2', 'b2', 'W1', 'b1', )}
    del _L3_conv_all

    return {
        "x": x,
        "L0_conv_weight": _L0_conv_in["weight"],
        "L1_conv_weights1": _L1_conv_in["weights1"],
        "L1_conv_weights2": _L1_conv_in["weights2"],
        "L2_conv_w1": _L2_conv_in["w1"],
        "L2_conv_b1": _L2_conv_in["b1"],
        "L2_conv_w2": _L2_conv_in["w2"],
        "L2_conv_b2": _L2_conv_in["b2"],
        "L3_conv_W2": _L3_conv_in["W2"],
        "L3_conv_b2": _L3_conv_in["b2"],
        "L3_conv_W1": _L3_conv_in["W1"],
        "L3_conv_b1": _L3_conv_in["b1"],
    }

def reference(x, L0_conv_weight, L1_conv_weights1, L1_conv_weights2, L2_conv_w1, L2_conv_b1, L2_conv_w2, L2_conv_b2, L3_conv_W2, L3_conv_b2, L3_conv_W1, L3_conv_b1):
    import jax
    import jax.numpy as jnp
    def _L0_conv_ref(x, weight):
        import jax, jax.numpy as jnp
        import numpy as np
        from jax import lax
        C_IN, C_OUT, K = (32, 32, 3)
        DIV = float(np.sqrt(C_IN * K * K))
        weight_bin = jnp.where(weight > 0, 1.0, -1.0).astype(weight.dtype)
        out = lax.conv_general_dilated(x, weight_bin, window_strides=(1, 1), padding=((K // 2, K // 2), (K // 2, K // 2)), dimension_numbers=('NCHW', 'OIHW', 'NCHW'))
        return out / DIV

    def _L1_conv_ref(x, weights1, weights2):
        import jax, jax.numpy as jnp
        import numpy as np
        B, C_IN, C_OUT, H, W, M1, M2 = (16, 32, 32, 256, 256, 16, 16)
        b, c_in, h, w = x.shape
        c_out, m1, m2 = (weights1.shape[1], weights1.shape[2], weights1.shape[3])
        x_ft = jnp.fft.rfft2(x)
        w1c = jax.lax.complex(weights1[..., 0], weights1[..., 1])
        corner = jnp.einsum('bixy,ioxy->boxy', x_ft[:, :, :m1, :m2], w1c)
        out_ft = jnp.zeros((b, c_out, h, w // 2 + 1), dtype=corner.dtype)
        out_ft = out_ft.at[:, :, :m1, :m2].set(corner)
        return jnp.fft.irfft2(out_ft, s=(h, w))

    def _L2_conv_ref(x, w1, b1, w2, b2):
        import jax, jax.numpy as jnp
        import numpy as np
        from jax import lax
        B, C, H, W = (16, 32, 384, 384)
        NK = 32
        K = 3
        HID = 128
        b, c, h, w = x.shape
        pooled = x.mean(axis=(2, 3))
        hdn = jax.nn.relu(pooled @ w1 + b1)
        kernels = (hdn @ w2 + b2).reshape(b, NK, K, K)
        xg = x[:, :NK].reshape(1, b * NK, h, w)
        wgt = kernels.reshape(b * NK, 1, K, K)
        pad = K // 2
        out = lax.conv_general_dilated(xg, wgt, window_strides=(1, 1), padding=[(pad, pad), (pad, pad)], feature_group_count=b * NK, dimension_numbers=('NCHW', 'OIHW', 'NCHW'))
        return out.reshape(b, NK, h, w)

    def _L3_conv_ref(x, W2, b2, W1, b1):
        import jax, jax.numpy as jnp
        import numpy as np
        BATCH, IN_DIM, H, W = (16, 32, 128, 128)
        BASE_OUT = 32
        b, c, h, w = x.shape
        bo = W1.shape[1]
        rows = jnp.arange(h)
        cols = rows[:, None] + jnp.arange(w)[None, :]
        skewed = jnp.zeros((b, c, h, 2 * w - 1), x.dtype).at[:, :, rows[:, None], cols].set(x)
        i2s = jnp.einsum('oc,bchy->bohy', W2, skewed) + b2[None, :, None, None]
        xs = jnp.moveaxis(i2s[:, :, :, :w], 3, 0)
        W1_prev, W1_cur = (W1[:, :, 0], W1[:, :, 1])

        def step(carry, xt):
            pc, ph = carry
            ph_shift = jnp.pad(ph, ((0, 0), (0, 0), (1, 0)))[:, :, :-1]
            s2s = jnp.einsum('oc,bch->boh', W1_prev, ph_shift) + jnp.einsum('oc,bch->boh', W1_cur, ph) + b1[None, :, None]
            g = xt + s2s
            o = jax.nn.sigmoid(g[:, 0 * bo:1 * bo])
            f = jax.nn.sigmoid(g[:, 1 * bo:2 * bo])
            i = jax.nn.sigmoid(g[:, 2 * bo:3 * bo])
            gg = jnp.tanh(g[:, 3 * bo:4 * bo])
            nc = f * pc + i * gg
            nh = o * jnp.tanh(nc)
            return ((nc, nh), nh)
        c0 = jnp.zeros((b, bo, h), x.dtype)
        _, hs = jax.lax.scan(step, (c0, c0), xs)
        return jnp.moveaxis(hs, 0, -1)

    def _gn(v, G=16, eps=1e-5):
        B_, C_, H_, W_ = v.shape
        g = v.reshape(B_, G, C_ // G, H_, W_)
        m = jnp.mean(g, axis=(2, 3, 4), keepdims=True)
        s = jnp.var(g, axis=(2, 3, 4), keepdims=True)
        return ((g - m) / jnp.sqrt(s + eps)).reshape(v.shape)

    def _ln_c(v, eps=1e-6):
        m = jnp.mean(v, axis=1, keepdims=True)
        s = jnp.var(v, axis=1, keepdims=True)
        return (v - m) / jnp.sqrt(s + eps)

    def _ln_t(v, eps=1e-5):
        m = jnp.mean(v, axis=-1, keepdims=True)
        s = jnp.var(v, axis=-1, keepdims=True)
        return (v - m) / jnp.sqrt(s + eps)

    def _to_tokens(v):
        B_, C_, H_, W_ = v.shape
        return v.reshape(B_, C_, H_ * W_).transpose(0, 2, 1)
    def _from_tokens(t, like):
        B_, C_, H_, W_ = like.shape
        return t.transpose(0, 2, 1).reshape(B_, C_, H_, W_)

    x = x + _L0_conv_ref(_gn(x), L0_conv_weight)
    x = x + _L1_conv_ref(_gn(x), L1_conv_weights1, L1_conv_weights2)
    x = x + _L2_conv_ref(_gn(x), L2_conv_w1, L2_conv_b1, L2_conv_w2, L2_conv_b2)
    x = x + _L3_conv_ref(_gn(x), L3_conv_W2, L3_conv_b2, L3_conv_W1, L3_conv_b1)
    return x


_drawn_inputs = setup_inputs


def setup_inputs(seed=0):
    import zlib

    import numpy as np

    out = dict(_drawn_inputs(seed))
    spreads = {'L2_conv_b1': (0.0, 0.1), 'L2_conv_b2': (0.0, 0.1)}
    factors = {'L1_conv_weights1': 64.0, 'L2_conv_w1': 8.0, 'L3_conv_W1': 3.815}
    for name, (base, spread) in spreads.items():
        noise = np.random.default_rng([zlib.crc32(name.encode()), seed]).standard_normal(out[name].shape)
        drawn = base * np.exp(spread * noise) if base else spread * noise
        out[name] = jnp.asarray(drawn.astype(out[name].dtype))
    for name, factor in factors.items():
        out[name] = (out[name] * factor).astype(out[name].dtype)
    return out
```

```python
from contextlib import ExitStack

import concourse.bass as bass
from concourse import mybir

F32 = mybir.dt.float32
ALU = mybir.AluOpType
ACT = mybir.ActivationFunctionType

NB, C, H, W = 16, 32, 256, 256
P = 128
S = P // C
KB = H // S
WP = W + 2
CK = 8
NCH = KB // CK
GK = 2
NG = CK // GK
NGI = NCH * NG
M = 16
MM = M * M
T = 16
PAD = 16
WX = PAD + W
EPS = 1e-5


DIV = float((C * 9) ** 0.5)
HC = 2 * NCH
HB = CK // 2


class Count:

    def __init__(self, base):
        self.base, self.n = base, 0

    def next(self):
        self.n += 1
        return self.base + self.n


def image_loop(eng, body):
    with eng.Fori(0, NB // 2 - 1) as i:
        for u in range(2):
            body(i * 2 + u, u, False, False)
    body(NB - 2, 0, False, True)
    body(NB - 1, 1, True, True)


def image(t, n):
    return t[bass.ds(n, 1)]


def conv_phase(nc, layer, src, dst, stats, spectra, const, par):
    second = layer == 2
    left = PAD if second else 0
    with ExitStack() as ctx:
        def sb(name, shape):
            return ctx.enter_context(nc.sbuf_tensor(f"{name}_l{layer}", shape, F32))

        def sem(name):
            return ctx.enter_context(nc.semaphore(f"{name}_l{layer}"))

        xa = [sb(f"xa{u}", [P, KB + 1, WP]) for u in range(2)]
        xb = [sb(f"xb{u}", [P, HB, WP]) for u in range(4)]
        xt = [sb(f"xt{u}", [P, WP]) for u in range(2)]
        oc = [sb(f"oc{u}", [P, HB, W]) for u in range(4)]
        ist = sb("ist", [P, NGI, 6])
        ost = sb("ost", [P, NGI, 6])
        agg_i = sb("agg_i", [P, 2])
        agg_o = sb("agg_o", [P, 2])
        grp_i = sb("grp_i", [P, 2])
        grp_o = sb("grp_o", [P, 2])
        scl = sb("scl", [P, 1])
        veps, root, inv, half = (sb(x, [P, 1]) for x in ("veps", "root", "inv", "half"))
        dev = sb("dev", [P, 1])
        var = sb("var", [P, 1])
        wn = sb("wn", [P, 3, 2, C])
        wf = [sb(f"wf{u}", [P, 3, 2, C]) for u in range(2)]
        nb = [sb(f"nb{u}", [P, 1]) for u in range(2)]
        ones = sb("ones", [P, WP])
        g8 = sb("g8", [P, P])
        i3 = sb("i3", [P, 3, 2, C])
        if not second:
            wraw = sb("wraw", [C, C, 3, 3])
            ident = sb("ident", [C, C])
            wb = sb("wb", [P, 3, 2, C])
        else:
            ident = sb("ident", [2 * C, 2 * C])
            g4 = sb("g4", [P, P])
            i4 = sb("i4", [P, C])
            w1 = sb("w1", [C, P])
            b1 = sb("b1", [P, 1])
            w2raw = sb("w2raw", [P, C, 3, 3])
            w2r = sb("w2r", [P, 3, 2, S, C])
            b2c = sb("b2c", [C, 3, 3])
            b2r = sb("b2r", [P, 3, 2])
            pool = sb("pool", [P, 1])
            hdn = sb("hdn", [P, 1])
            kern = sb("kern", [P, 6])
            kn = sb("kn", [P, 6])
            mpad = sb("mpad", [P, PAD])
            mpads = sb("mpads", [P, KB, PAD])
            o1 = [sb(f"o1{u}", [2 * C, M, M]) for u in range(2)]
            tt = sb("tt", [2 * C, C, 2, M])
            eh = sb("eh", [2 * C, H])
            ew = sb("ew", [C, W])
            gs = sb("gs", [C, H // 2, C])

        cps = ctx.enter_context(nc.psum_tensor(f"cps_l{layer}", [P, 4, GK, W], F32))
        yps = ctx.enter_context(nc.psum_tensor(f"yps_l{layer}", [P, 3, GK, W], F32))
        sm = ctx.enter_context(nc.psum_tensor(f"sm_l{layer}", [P, 512], F32))

        passed = sem("passed")
        setup = sem("setup")
        turned = sem("turned")
        ready = sem("ready")
        xa_loaded = [sem(f"xa_loaded{u}") for u in range(2)]
        xa_final = sem("xa_final")
        taps_ready = sem("taps_ready")
        xb_loaded = [sem(f"xb_loaded{u}") for u in range(4)]
        xt_loaded = [sem(f"xt_loaded{u}") for u in range(2)]
        conv_ready = sem("conv_ready")
        evac = sem("evac")
        ostat = sem("ostat")
        istat = sem("istat")
        stored = [sem(f"stored{u}") for u in range(4)]
        link = sem("link")
        v2p = sem("v2p")
        p2v = sem("p2v")
        var_ready = sem("var_ready")
        root_ready = sem("root_ready")
        nb_ready = sem("nb_ready")
        grp_ready = sem("grp_ready")
        grp_stored = sem("grp_stored")
        o1_loaded = [sem(f"o1_loaded{u}") for u in range(2)]
        t_ready = sem("t_ready")
        t_copied = sem("t_copied")
        g_ready = sem("g_ready")
        g_copied = sem("g_copied")
        y_ready = sem("y_ready")
        y_added = sem("y_added")

        K_IN = 5 if second else 3
        K = K_IN + 2
        N_SETUP = 16 * (12 if second else 4)
        banks_of = [0] * 3 + [4] * 4 + [0] * 2 + [4] * 4 + [0] * 3 if second else [3] * 8 + [2] * 4 + [0] * 4
        spectra_at = {1: (0, 0, 4), 2: (0, 4, 8), 7: (1, 0, 4), 8: (1, 4, 8)}
        starts = [sum(banks_of[:h]) for h in range(HC)]

        def load_image(eng, n, u):
            for s in range(S):
                rows = image(src, n).rearrange("b c (k s) w -> s (b c) k w", s=S)[s]
                eng.dma_start(xa[u][C * s:C * (s + 1), 0:KB, 1:W + 1], rows).then_inc(xa_loaded[u], 16)

        block = ctx.enter_context(nc.Block(name=f"conv{layer}"))

        @block.sync
        def _(sp):
            for o in range(4):
                sp.sem_inc(stored[o], 1)
            sp.sem_inc(grp_stored, 1)
            load_image(sp, 0, 0)
            sp.dma_start(g8[:], const["g8"]).then_inc(setup, 16)
            sp.dma_start(i3[:], const["i3"].rearrange("p (a b c) -> p a b c", a=3, b=2)).then_inc(setup, 16)
            n_id = 2 * C if second else C
            sp.dma_start(ident[:], const["ident"][0:n_id, 0:n_id]).then_inc(setup, 16)
            if not second:
                sp.dma_start(wraw[:], par["w"]).then_inc(setup, 16)
            else:
                sp.dma_start(g4[:], const["g4"]).then_inc(setup, 16)
                sp.dma_start(i4[:], const["i4"]).then_inc(setup, 16)
                sp.dma_start(eh[:], const["eh"]).then_inc(setup, 16)
                sp.dma_start(ew[:], const["ew"]).then_inc(setup, 16)
                sp.dma_start(w1[:], par["w1"]).then_inc(setup, 16)
                sp.dma_start(b1[:], par["b1"].rearrange("(a b) -> a b", b=1)).then_inc(setup, 16)
                sp.dma_start(w2raw[:], par["w2"].rearrange("p (c h w) -> p c h w", h=3, w=3)).then_inc(setup, 16)
                sp.dma_start(mpad[:], const["ones"][:, 0:PAD]).then_inc(setup, 16)
                sp.dma_start(b2c[:], par["b2"].rearrange("(c h w) -> c h w", h=3, w=3)).then_inc(setup, 16)
            load_image(sp, 1, 1)

            def body(n, u, last, tail):
                for h in range(HC):
                    sp.wait_ge(evac, n * NGI + 4 + 2 * (h + 1))
                    o = h % 4
                    for s in range(S):
                        blocks = HB - (h == HC - 1 and s == S - 1)
                        r0 = h * HB * S + 1 + s
                        rows = image(dst, n)[:, :, r0:r0 + (blocks - 1) * S + 1:S, left:left + W]
                        sp.dma_start(rows.rearrange("b c k w -> (b c) k w"),
                                     oc[o][C * s:C * (s + 1), 0:blocks, :]).then_inc(stored[o], 16)
                    if h == HC - 1:
                        row = image(dst, n)[:, :, 0:1, left:left + W]
                        sp.dma_start(row.rearrange("b c k w -> (b c) k w"),
                                     oc[o][3 * C:P, HB - 1:HB, :]).then_inc(stored[o], 16)
                sp.wait_ge(grp_ready, n + 1)
                sp.dma_start(image(stats, n).rearrange("b c s -> (b c) s"), grp_o[0:C, :]).then_inc(grp_stored, 16)
                if second:
                    for s in range(S):
                        cells = image(dst, n).rearrange("b c (k s) w -> s (b c) k w", s=S)[s][:, :, 0:PAD]
                        sp.dma_start(cells, mpads[C * s:C * (s + 1)]).then_inc(grp_stored, 16)
                if tail:
                    return
                sp.wait_ge(conv_ready, (n + 1) * NGI + 8)
                load_image(sp, n + 2, u)

            image_loop(sp, body)
            for o in range(4):
                sp.wait_ge(stored[o], NB * 16 * (4 * S + (o == 3)) + 1)
            sp.wait_ge(grp_stored, NB * 16 * (1 + S * second) + 1)

        @block.gpsimd
        def _(pl):
            if second:
                for u in range(2):
                    pl.dma_start(o1[u][:], spectra[u].rearrange("p (x y) -> p x y", y=M)).then_inc(o1_loaded[u], 16)

            def body(n, u, last, tail):
                pl.wait_ge(xa_final, n + 1)
                pl.sem_inc(passed, 1)
                pl.dma_start(xt[u][2 * C:P, :], xa[u][0:2 * C, 0, :]).then_inc(xt_loaded[u], 16)
                for h in range(HC):
                    pl.wait_ge(conv_ready, n * NGI + 2 * h + 2)
                    pl.sem_inc(passed, 1)
                    k = HB * h
                    pl.dma_start(xb[h % 4][0:2 * C], xa[u][2 * C:P, k:k + HB, :]).then_inc(xb_loaded[h % 4], 16)
                    pl.dma_start(xb[h % 4][2 * C:P], xa[u][0:2 * C, k + 1:k + HB + 1, :]).then_inc(xb_loaded[h % 4], 16)
                if second and not tail:
                    pl.wait_ge(t_ready, n + 1)
                    pl.sem_inc(passed, 1)
                    pl.dma_start(o1[u][:], image(spectra, n + 2).rearrange("b p (x y) -> (b p) x y", y=M)).then_inc(o1_loaded[u], 16)
            image_loop(pl, body)

        @block.tensor
        def _(pe):
            def input_norm(c):
                pe.wait_ge(v2p, c.next())
                if second:
                    nc.tensor.matmul(sm[:, 2:3], g4[:], agg_i[:, 0:1], start=True, stop=True)
                nc.tensor.matmul(sm[:, 0:1], g8[:], agg_i[:, 0:1], start=True, stop=True).then_inc(p2v, 1)
                pe.wait_ge(v2p, c.next())
                nc.tensor.matmul(sm[:, 1:2], g8[:], var[:], start=True, stop=True).then_inc(p2v, 1)

            def output_norm(c):
                pe.wait_ge(v2p, c.next())
                nc.tensor.matmul(sm[:, 0:1], g8[:], agg_o[:, 0:1], start=True, stop=True).then_inc(p2v, 1)
                pe.wait_ge(v2p, c.next())
                nc.tensor.matmul(sm[:, 1:2], g8[:], var[:], start=True, stop=True).then_inc(p2v, 1)

            def taps(c):
                if second:
                    pe.wait_ge(v2p, c.next())
                    nc.tensor.matmul(sm[:, 3:4], w1[:], pool[0:C, :], start=True, stop=True).then_inc(p2v, 1)
                    pe.wait_ge(v2p, c.next())
                    for t in range(6):
                        ins = nc.tensor.matmul(sm[:, 4 + t:5 + t], w2r[:, t // 2, t % 2], hdn[:], start=True, stop=True)
                    ins.then_inc(p2v, 1)
                pe.wait_ge(v2p, c.next())
                for t in range(2):
                    for dw in range(3):
                        ins = nc.tensor.matmul(sm[2 * C * t:2 * C * (t + 1), 10:11], wn[:, dw], grp_i[:, 0:1],
                                               start=dw == 0, stop=dw == 2)
                ins.then_inc(p2v, 1)

            def conv_bank(n, u, h, g):
                b = (2 * h + g) % 4
                pe.wait_ge(evac, n * NGI + 2 * h + g + 1)
                k = HB * h + GK * g
                end = h == HC - 1 and g == 1
                copy_b = xb[h % 4][:, GK * g:GK * (g + 1)]
                for dw in range(3):
                    f = dict(start=dw == 0, stop=dw == 2)
                    ins = nc.tensor.matmul(cps[0:2 * C, b], wf[u][:, dw], xa[u][:, k:k + GK, dw:dw + W], **f)
                    if not end:
                        ins = nc.tensor.matmul(cps[2 * C:P, b], wf[u][:, dw], copy_b[:, :, dw:dw + W], **f)
                if end:
                    for dw in range(3):
                        nc.tensor.matmul(cps[2 * C:P, b, 0], wf[u][:, dw], copy_b[:, 0, dw:dw + W],
                                         start=dw == 0, stop=dw == 2)
                    for dw in range(3):
                        nc.tensor.matmul(cps[2 * C:3 * C, b, 1], wf[u][:, dw, 0], copy_b[:, 1, dw:dw + W],
                                         start=dw == 0, stop=dw == 2)
                    for dw in range(3):
                        ins = nc.tensor.matmul(cps[3 * C:P, b, 1], wf[u][:, dw, 1], xt[u][:, dw:dw + W],
                                               start=dw == 0, stop=dw == 2)
                ins.then_inc(conv_ready, 1)

            def turn_modes(n, u):
                pe.wait_ge(o1_loaded[u], (n - u) * 8 + 16)
                pe.wait_ge(y_added, n * NGI + 1)
                pe.sem_inc(passed, 1)
                for ky in range(M):
                    bank = yps[0:M, ky // 8].rearrange("p a b -> p (a b)")
                    ins = nc.tensor.transpose(bank[:, 64 * (ky % 8):64 * (ky % 8) + 64], o1[u][:, :, ky], ident[:])
                ins.then_inc(t_ready, 1)

            def row_spectra(n, half, q0, q1):
                for q in range(q0, q1):
                    if q == 0:
                        pe.wait_ge(t_copied, n + 1)
                        pe.wait_ge(y_added, n * NGI + half * NGI // 2 + 1)
                    if q >= 3:
                        pe.wait_ge(g_copied, n * 16 + half * 8 + q - 2)
                    nc.tensor.matmul(yps[:, q % 3, 0, 0:H // 2], tt[:, 4 * q:4 * q + 4], eh[:, half * H // 2:(half + 1) * H // 2],
                                     start=True, stop=True).then_inc(g_ready, 1)

            def inverse_bank(n, g):
                if g % (NGI // 2) == 0:
                    pe.wait_ge(g_copied, n * 16 + 8 * (g // (NGI // 2)) + 8)
                if g >= 3:
                    pe.wait_ge(y_added, n * NGI + g - 1)
                for r in range(GK):
                    row = (GK * g + r) * S % (H // 2)
                    ins = nc.tensor.matmul(yps[:, g % 3, r], gs[:, row:row + S], ew[:], start=True, stop=True)
                ins.then_inc(y_ready, 1)

            pe.sem_inc(conv_ready, 8)
            pe.wait_ge(setup, N_SETUP)
            if not second:
                for t in range(9):
                    ins = nc.tensor.transpose(sm[0:C, C * t:C * (t + 1)], wraw[:, :, t // 3, t % 3], ident[:])
                ins.then_inc(turned, 1)
            pe.wait_ge(ready, 1)
            if second:
                turn_modes(0, 0)
                for half in range(2):
                    row_spectra(0, half, 0, 8)
                    for g in range(NGI // 2):
                        inverse_bank(0, NGI // 2 * half + g)
            c = Count(0)
            input_norm(c)
            taps(c)

            def body(n, u, last, tail):
                c = Count(K_IN + n * K)
                for h in range(HC):
                    if second and not last and h == 0:
                        turn_modes(n + 1, 1 - u)
                    if second and not last and h in spectra_at:
                        row_spectra(n + 1, *spectra_at[h])
                    if h == 0:
                        pe.wait_ge(taps_ready, n + 1)
                    pe.wait_ge(xb_loaded[h % 4], n * 128 + (h // 4 + 1) * 32)
                    if h == HC - 1:
                        pe.wait_ge(xt_loaded[u], (n - u) * 8 + 16)
                    for g in range(2):
                        conv_bank(n, u, h, g)
                        if second and not last:
                            for gg in range(banks_of[h] // 2):
                                inverse_bank(n + 1, starts[h] + banks_of[h] // 2 * g + gg)
                    if h == 13 and not last:
                        input_norm(c)
                        taps(c)
                output_norm(c)
            image_loop(pe, body)

        @block.scalar
        def _(act):
            def copy_modes(n):
                act.wait_ge(t_ready, n + 1)
                for b in range(2):
                    v = yps[0:M, b].rearrange("p a b -> p (a b)").rearrange("p (y r o) -> p r o y", r=2, o=C)
                    y = slice(8 * b, 8 * b + 8)
                    for r in range(2):
                        nc.scalar.activation(tt[0:M, :, r, y], v[:, r], ACT.Copy)
                    nc.scalar.activation(tt[C:C + M, :, 0, y], v[:, 1], ACT.Copy, scale=-1.0)
                    ins = nc.scalar.activation(tt[C:C + M, :, 1, y], v[:, 0], ACT.Copy)
                ins.then_inc(t_copied, 1)

            def copy_spectra(n, half, q0, q1):
                for q in range(q0, q1):
                    act.wait_ge(g_ready, n * 16 + half * 8 + q + 1)
                    for o in range(4):
                        ins = nc.scalar.activation(gs[:, :, 4 * q + o], yps[C * o:C * (o + 1), q % 3, 0, 0:H // 2], ACT.Copy)
                    ins.then_inc(g_copied, 1)

            def root_of(n):
                act.wait_ge(var_ready, n + 1)
                nc.scalar.activation(root[:], veps[:], ACT.Sqrt).then_inc(root_ready, 1)

            act.sem_inc(evac, 4)
            act.wait_ge(ready, 1)
            if second:
                copy_modes(0)
                for half in range(2):
                    copy_spectra(0, half, 0, 8)
            root_of(0)

            def body(n, u, last, tail):
                act.wait_ge(nb_ready, n + 1)
                for h in range(HC):
                    o = h % 4
                    if second and not last and h in spectra_at:
                        copy_spectra(n + 1, *spectra_at[h])
                    act.wait_ge(stored[o], n * 16 * (4 * S + (o == 3)) + 16 * S * (h // 4) + 1)
                    act.wait_ge(ostat, n * HC + h + 1)
                    for g in range(2):
                        act.wait_ge(conv_ready, n * NGI + 8 + 2 * h + g + 1)
                        nc.scalar.activation(oc[o][:, GK * g:GK * (g + 1)], cps[:, (2 * h + g) % 4], ACT.Identity,
                                             bias=nb[u][:, 0:1]).then_inc(evac, 1)
                    if h == 13 and not last:
                        root_of(n + 1)
                    if second and not last and h == 0:
                        copy_modes(n + 1)
            image_loop(act, body)

        @block.vector
        def _(dve):
            v = nc.vector

            def chained(c, ins):
                ins.then_inc(link, 1)
                dve.wait_ge(link, c.next())

            c = Count(0)
            dve.sem_inc(ostat, 4)
            dve.sem_inc(y_added, 1)
            v.memset(ones[:], 1.0)
            for u in range(2):
                v.memset(xa[u][2 * C:P, KB, :], 0.0)
            if not second:
                chained(c, v.memset(wb[:], 0.0))
                dve.wait_ge(turned, 1)
                w = sm[0:C, 0:9 * C].rearrange("p (h w o) -> p h w o", h=3, w=3)
                for i in range(2):
                    for kh in range(3):
                        j = i + kh
                        ins = v.tensor_scalar(wb[C * j:C * (j + 1), :, i, :], w[:, kh], 0.0, 2.0 / DIV, ALU.is_gt, ALU.mult)
                chained(c, ins)
                for i in range(2):
                    for kh in range(3):
                        j = i + kh
                        cells = wb[C * j:C * (j + 1), :, i, :]
                        ins = v.tensor_scalar(cells, cells, -1.0 / DIV, None, ALU.add)
                chained(c, ins)
            else:
                v.memset(b2r[:], 0.0)
                v.memset(tt[:], 0.0)
                chained(c, v.memset(w2r[:], 0.0))
                dve.wait_ge(setup, N_SETUP)
                for i in range(2):
                    for kh in range(3):
                        for kw in range(3):
                            v.tensor_copy(w2r[:, kw, i, i + kh, :], w2raw[:, :, kh, kw])
                        j = i + kh
                        ins = v.tensor_copy(b2r[C * j:C * (j + 1), :, i], b2c[:, kh, :])
                chained(c, ins)
            dve.sem_inc(ready, 1)
            dve.wait_ge(setup, N_SETUP)

            def input_banks(n, u, g0, g1):
                for g in range(g0, g1):
                    cells = xa[u][:, GK * g:GK * (g + 1), 1:W + 1]
                    if g == 0:
                        dve.wait_ge(xa_loaded[u], (n - u) * 32 + 64)
                    if second:
                        dve.wait_ge(y_ready, n * NGI + g + 1)
                        v.tensor_tensor(cells, cells, yps[:, g % 3], ALU.add).then_inc(y_added, 1)
                        dve.wait_ge(y_added, n * NGI + g + 2)
                    ins = v.bn_stats(ist[:, g, :], cells)
                    if g == NGI - 1:
                        ins.then_inc(istat, 1)

            def norm(c, cp, agg, st, grp):
                v.bn_aggr(agg[:], st[:].rearrange("p g s -> p (g s)")).then_inc(v2p, 1)
                dve.wait_ge(p2v, cp.next())
                v.tensor_copy(grp[:, 0:1], sm[:, 0:1])
                chained(c, v.tensor_tensor(dev[:], agg[:, 0:1], sm[:, 0:1], ALU.subtract))
                v.scalar_tensor_tensor(out=var[:], in0=dev[:], scalar=dev[:, 0:1], in1=agg[:, 1:2],
                                       op0=ALU.mult, op1=ALU.add).then_inc(v2p, 1)
                dve.wait_ge(p2v, cp.next())
                return v.tensor_copy(grp[:, 1:2], sm[:, 1:2])

            def input_norm(c, cp, n):
                dve.wait_ge(istat, n + 1)
                dve.sem_inc(passed, 1)
                norm(c, cp, agg_i, ist, grp_i)
                chained(c, v.tensor_scalar(veps[:], sm[:, 1:2], EPS, None, ALU.add))
                dve.sem_inc(var_ready, 1)
                dve.wait_ge(root_ready, n + 1)
                chained(c, v.reciprocal(inv[:], root[:]))
                chained(c, v.scalar_tensor_tensor(out=half[:], in0=inv[:], scalar=inv[:, 0:1], in1=veps[:],
                                                  op0=ALU.mult, op1=ALU.mult))
                chained(c, v.tensor_scalar(half[:], half[:], -0.5, 1.5, ALU.mult, ALU.add))
                chained(c, v.tensor_tensor(scl[:], inv[:], half[:], ALU.mult))

            def taps(c, cp, n, u):
                mean, scale = grp_i[:, 0:1], scl[:, 0:1]
                taps6 = wn[:].rearrange("p a b o -> p (a b) o")
                if not second:
                    v.tensor_scalar(wn[:], wb[:], scale, None, ALU.mult).then_inc(v2p, 1)
                else:
                    v.tensor_scalar(pool[:], sm[:, 2:3], mean, scale, ALU.subtract, ALU.mult).then_inc(v2p, 1)
                    dve.wait_ge(p2v, cp.next())
                    v.tensor_scalar(hdn[:], sm[:, 3:4], b1[:, 0:1], 0.0, ALU.add, ALU.max).then_inc(v2p, 1)
                    dve.wait_ge(p2v, cp.next())
                    chained(c, v.tensor_tensor(kern[:], sm[:, 4:10], b2r[:].rearrange("p a b -> p (a b)"), ALU.add))
                    chained(c, v.tensor_scalar(kn[:], kern[:], scale, None, ALU.mult))
                    for t in range(6):
                        ins = v.tensor_scalar(taps6[:, t, :], i4[:], kn[:, t:t + 1], None, ALU.mult)
                    ins.then_inc(v2p, 1)
                v.tensor_scalar(xa[u][:, 0:KB, 0:W + 2:W + 1], ones[:, 0:2 * KB].rearrange("p (a b) -> p a b", b=2),
                                mean, None, ALU.mult)
                v.tensor_scalar(xt[u][0:2 * C, :], ones[0:2 * C, :], grp_i[0:2 * C, 0:1], None, ALU.mult)
                v.tensor_scalar(xa[u][0:2 * C, KB, :], ones[0:2 * C, :], grp_i[0:2 * C, 0:1], None,
                                ALU.mult).then_inc(xa_final, 1)
                dve.wait_ge(p2v, cp.next())
                v.tensor_tensor(wf[u][:], wn[:], i3[:], ALU.add).then_inc(taps_ready, 1)
                v.tensor_scalar(nb[u][:], sm[:, 10:11], -1.0, None, ALU.mult).then_inc(nb_ready, 1)

            input_banks(0, 0, 0, NGI)
            cp = Count(0)
            input_norm(c, cp, 0)
            taps(c, cp, 0, 0)
            c0 = c.n
            links = 10 if second else 8

            def body(n, u, last, tail):
                c, cp = Count(c0 + n * links), Count(K_IN + n * K)
                for h in range(HC):
                    if not last:
                        input_banks(n + 1, 1 - u, starts[h], starts[h] + banks_of[h])
                    dve.wait_ge(evac, n * NGI + 4 + 2 * (h + 1))
                    for g in range(2):
                        ins = v.bn_stats(ost[:, 2 * h + g, :], oc[h % 4][:, GK * g:GK * (g + 1)])
                    ins.then_inc(ostat, 1)
                    if h == 12 and not last:
                        input_norm(c, cp, n + 1)
                        taps(c, cp, n + 1, 1 - u)
                dve.wait_ge(ostat, (n + 1) * HC + 4)
                dve.wait_ge(grp_stored, n * 16 * (1 + S * second) + 1)
                dve.sem_inc(passed, 1)
                chained(c, norm(c, cp, agg_o, ost, grp_o))
                assert last or c.n == links
                if second:
                    chained_ = v.tensor_scalar(mpads[:], mpad[:].unsqueeze(1).broadcast_to([P, KB, PAD]), grp_o[:, 0:1], None, ALU.mult)
                    chained_.then_inc(grp_ready, 1)
                else:
                    dve.sem_inc(grp_ready, 1)
            image_loop(dve, body)


def spectrum_phase(nc, src, spectra, const):
    with ExitStack() as ctx:
        def sb(name, shape):
            return ctx.enter_context(nc.sbuf_tensor(f"{name}_sp", shape, F32))

        def sem(name):
            return ctx.enter_context(nc.semaphore(f"{name}_sp"))

        xh = [sb(f"xh{u}", [P, 2, C, W]) for u in range(2)]
        col = sb("col", [P, 4, 2 * W])
        turn = sb("turn", [P, 2, 8, P])
        xs = [sb(f"xs{u}", [2 * C, M, M]) for u in range(2)]
        fh = sb("fh", [P, 2, 2 * M])
        fw = sb("fw", [P, 2, 2, 2 * M])
        ident = sb("ident", [P, P])
        cp_ = ctx.enter_context(nc.psum_tensor("cp_sp", [P, 4, 512], F32))
        tp = ctx.enter_context(nc.psum_tensor("tp_sp", [P, 4, 4, P], F32))

        setup = sem("setup")
        loaded = [sem(f"loaded{u}") for u in range(2)]
        col_ready = sem("col_ready")
        col_act = sem("col_act")
        col_dve = sem("col_dve")
        turn_ready = sem("turn_ready")
        turn_act = sem("turn_act")
        turn_dve = sem("turn_dve")
        modes_ready = sem("modes_ready")
        modes_act = sem("modes_act")
        modes_dve = sem("modes_dve")
        stored = [sem(f"stored{u}") for u in range(2)]

        block = ctx.enter_context(nc.Block(name="spectrum"))

        def load_image(eng, n, u):
            for half in range(2):
                rows = image(src, n).rearrange("b c (f p) w -> f p (b c) w", f=2)[half]
                eng.dma_start(xh[u][:, half], rows).then_inc(loaded[u], 16)

        @block.sync
        def _(sp):
            for u in range(2):
                sp.sem_inc(stored[u], 1)
            load_image(sp, 0, 0)
            sp.dma_start(fh[:], const["fh"].rearrange("p (a b) -> p a b", a=2)).then_inc(setup, 16)
            sp.dma_start(fw[:], const["fw"].rearrange("p (a b c) -> p a b c", a=2, b=2)).then_inc(setup, 16)
            sp.dma_start(ident[:], const["ident"]).then_inc(setup, 16)
            load_image(sp, 1, 1)

            def body(n, u, last, tail):
                if not tail:
                    sp.wait_ge(col_ready, (n + 1) * 4)
                    load_image(sp, n + 2, u)
                sp.wait_ge(modes_act, n + 2)
                sp.wait_ge(modes_dve, n + 2)
                sp.dma_start(image(spectra, n).rearrange("b p (x y) -> (b p) x y", y=M), xs[u][:]).then_inc(stored[u], 16)
            image_loop(sp, body)
            for u in range(2):
                sp.wait_ge(stored[u], NB // 2 * 16 + 1)

        @block.tensor
        def _(pe):
            pe.wait_ge(setup, 48)

            def body(n, u, last, tail):
                pe.wait_ge(loaded[u], (n - u) * 16 + 32)
                pe.wait_ge(modes_act, n + 1)
                pe.wait_ge(modes_dve, n + 1)
                for nb in range(4):
                    for q in range(4):
                        for half in range(2):
                            first = 8 * nb + q
                            ins = nc.tensor.matmul(cp_[C * q:C * (q + 1), nb], fh[:, half], xh[u][:, half, first:first + 5:4, :],
                                                   start=half == 0, stop=half == 1)
                    ins.then_inc(col_ready, 1)
                for half in range(2):
                    for j in range(8):
                        if half == 0 and j == 0:
                            pe.wait_ge(col_act, 2 * n + 2)
                            pe.wait_ge(turn_act, 2 * n + 1)
                            pe.wait_ge(turn_dve, 2 * n + 1)
                        if half == 0 and j == 4:
                            pe.wait_ge(col_dve, 2 * n + 2)
                        at = (j % 2) * W + half * P
                        ins = nc.tensor.transpose(tp[:, 2 * half + j // 4, j % 4], col[:, j // 2, at:at + P], ident[:])
                        if j % 4 == 3:
                            ins.then_inc(turn_ready, 1)
                for kx in range(M):
                    for half in range(2):
                        if kx == 0:
                            pe.wait_ge(turn_act if half == 0 else turn_dve, 2 * n + 3)
                        for r in range(2):
                            lhs = turn[:, half].rearrange("p j (q r k) -> p (j q) (r k)", q=4, r=2)[:, :, r * M + kx]
                            ins = nc.tensor.matmul(cp_[0:C, 0, 2 * M * kx:2 * M * (kx + 1)], lhs, fw[:, half, r],
                                                   start=half == 0 and r == 0, stop=half == 1 and r == 1)
                ins.then_inc(modes_ready, 1)
            image_loop(pe, body)

        def evacuate(eng, copy, mine, col_done, turn_done, modes_done):
            eng.sem_inc(turn_done, 1)
            eng.sem_inc(modes_done, 1)

            def body(n, u, last, tail):
                for k in range(2):
                    nb = 2 * mine + k
                    eng.wait_ge(col_ready, 4 * n + nb + 1)
                    copy(col[:, nb], cp_[:, nb]).then_inc(col_done, 1)
                for k in range(2):
                    eng.wait_ge(turn_ready, 4 * n + 2 * mine + k + 1)
                    copy(turn[:, mine, 4 * k:4 * k + 4], tp[:, 2 * mine + k]).then_inc(turn_done, 1)
                if mine:
                    eng.wait_ge(modes_act, n + 2)
                eng.wait_ge(modes_ready, n + 1)
                eng.wait_ge(stored[u], (n - u) * 8 + 1)
                modes = cp_[0:C, 0].rearrange("p (x r y) -> p r x y", r=2, y=M)
                copy(xs[u][C * mine:C * (mine + 1)], modes[:, mine]).then_inc(modes_done, 1)
            image_loop(eng, body)

        @block.scalar
        def _(act):
            evacuate(act, lambda o, i: nc.scalar.activation(o, i, ACT.Copy), 0, col_act, turn_act, modes_act)

        @block.vector
        def _(dve):
            evacuate(dve, lambda o, i: nc.vector.tensor_copy(o, i), 1, col_dve, turn_dve, modes_dve)


def mixing_phase(nc, spectra, stats, weights, mixed):
    with ExitStack() as ctx:
        def sb(name, shape):
            return ctx.enter_context(nc.sbuf_tensor(f"{name}_mx", shape, F32))

        def sem(name):
            return ctx.enter_context(nc.semaphore(f"{name}_mx"))

        wm = sb("wm", [2 * C, C, MM, 2])
        wr = sb("wr", [2 * C, C, MM, 2])
        x = sb("x", [2 * C, NB, MM])
        o = sb("o", [2 * C, NB, MM])
        st = sb("st", [2 * C, NB, 2])
        veps, root, inv, half, scl = (sb(n, [2 * C, NB]) for n in ("veps", "root", "inv", "half", "scl"))
        ps = ctx.enter_context(nc.psum_tensor("ps_mx", [2 * C, 8, 32, 16], F32))
        loaded = sem("loaded")
        w_loaded = sem("w_loaded")
        link = sem("link")
        root_ready = sem("root_ready")
        x_ready = sem("x_ready")
        w_act = sem("w_act")
        w_dve = sem("w_dve")
        ready = sem("ready")
        o_act = sem("o_act")
        o_dve = sem("o_dve")
        stored = sem("stored")
        block = ctx.enter_context(nc.Block(name="mixing"))

        @block.sync
        def _(sp):
            sp.dma_start(x[:], spectra.rearrange("b p m -> p b m")).then_inc(loaded, 16)
            for r in range(2):
                sp.dma_start(st[C * r:C * (r + 1)], stats.rearrange("b c s -> c b s")).then_inc(loaded, 16)
            w = weights.rearrange("i o x y r -> i o (x y) r")
            for part in range(4):
                of = slice(8 * part, 8 * part + 8)
                sp.dma_start(wr[C:2 * C, of], w[:, of]).then_inc(w_loaded, 16)
                sp.dma_start(wm[0:C, of], w[:, of]).then_inc(w_loaded, 16)
            sp.wait_ge(o_act, 4)
            sp.wait_ge(o_dve, 4)
            sp.dma_start(mixed.rearrange("b p m -> p b m"), o[:]).then_inc(stored, 16)
            sp.wait_ge(stored, 16)

        @block.vector
        def _(dve):
            v = nc.vector
            dve.wait_ge(loaded, 48)
            v.tensor_scalar(veps[:], st[:, :, 1], EPS, None, ALU.add).then_inc(link, 1)
            v.scalar_tensor_tensor(out=x[0:C, :, 0], in0=st[0:C, :, 0], scalar=-float(H * W), in1=x[0:C, :, 0],
                                   op0=ALU.mult, op1=ALU.add)
            dve.wait_ge(root_ready, 1)
            v.reciprocal(inv[:], root[:]).then_inc(link, 1)
            dve.wait_ge(link, 2)
            v.tensor_tensor(half[:], inv[:], inv[:], ALU.mult).then_inc(link, 1)
            dve.wait_ge(link, 3)
            v.tensor_tensor(half[:], half[:], veps[:], ALU.mult).then_inc(link, 1)
            dve.wait_ge(link, 4)
            v.tensor_scalar(half[:], half[:], -0.5, 1.5, ALU.mult, ALU.add).then_inc(link, 1)
            dve.wait_ge(link, 5)
            v.tensor_tensor(scl[:], inv[:], half[:], ALU.mult).then_inc(link, 1)
            dve.wait_ge(link, 6)
            v.tensor_tensor(x[:], x[:], scl[:].unsqueeze(2).broadcast_to([2 * C, NB, MM]), ALU.mult).then_inc(x_ready, 1)
            dve.wait_ge(w_loaded, 128)
            v.tensor_copy(wm[C:2 * C, :, :, 1], wr[C:2 * C, :, :, 0]).then_inc(w_dve, 1)
            for k in range(1, 8, 2):
                dve.wait_ge(ready, k + 1)
                v.tensor_copy(o[:, :, 32 * k:32 * k + 32], ps[:, k, :, 0:NB].rearrange("p m b -> p b m")).then_inc(o_dve, 1)

        @block.scalar
        def _(act):
            act.wait_ge(link, 1)
            nc.scalar.activation(root[:], veps[:], ACT.Sqrt).then_inc(root_ready, 1)
            act.wait_ge(w_loaded, 128)
            nc.scalar.activation(wm[C:2 * C, :, :, 0], wr[C:2 * C, :, :, 1], ACT.Copy, scale=-1.0).then_inc(w_act, 1)
            for k in range(0, 8, 2):
                act.wait_ge(ready, k + 1)
                nc.scalar.activation(o[:, :, 32 * k:32 * k + 32], ps[:, k, :, 0:NB].rearrange("p m b -> p b m"), ACT.Copy).then_inc(o_act, 1)

        @block.tensor
        def _(pe):
            pe.wait_ge(w_act, 1)
            pe.wait_ge(w_dve, 1)
            pe.wait_ge(x_ready, 1)
            for m in range(MM):
                for r in range(2):
                    ins = nc.tensor.matmul(ps[C * r:C * (r + 1), m // 32, m % 32, 0:NB], wm[:, :, m, r], x[:, :, m],
                                           start=True, stop=True)
                if m % 32 == 31:
                    ins.then_inc(ready, 1)


GH = 2
GB = S
STEPS = W
BLOCKS = STEPS // T
OUT, FORGET, IN, CELL = range(4)


def lstm_phase(nc, src, out, stats, par, const):
    with ExitStack() as ctx:
        def sb(name, shape):
            return ctx.enter_context(nc.sbuf_tensor(f"{name}_ls", shape, F32))

        def sem(name):
            return ctx.enter_context(nc.semaphore(f"{name}_ls"))

        def sems(name):
            return [sem(f"{name}{k}") for k in range(2)]

        xs = [sb(f"xs{k}", [P, GH, H, T]) for k in range(2)]
        ys = [sb(f"ys{k}", [P, GH, H, T]) for k in range(2)]
        hid = sb("hid", [P, GH, H + 1])
        cell = sb("cell", [P, GH, H])
        gate = sb("gate", [P, GH, 4, H])
        fc, ig, tc = (sb(n, [P, GH, H]) for n in ("fc", "ig", "tc"))
        below = sb("below", [P, GH, T])
        w2d = sb("w2d", [P, 4, P])
        w2n = sb("w2n", [P, GH, 4, P])
        w1d = sb("w1d", [P, 2, 4, P])
        w2raw = sb("w2raw", [P, C])
        w1raw = sb("w1raw", [P, C, 2])
        b1row, b2row, brow = (sb(n, [4, C]) for n in ("b1row", "b2row", "brow"))
        b12 = sb("b12", [P, 4])
        bias = sb("bias", [P, GH, 4])
        st = sb("st", [P, GH, 2])
        veps, root, inv, half, scl = (sb(n, [P, GH]) for n in ("veps", "root", "inv", "half", "scl"))
        ident = sb("ident", [P, P])
        ps = ctx.enter_context(nc.psum_tensor("ps_ls", [P, GH, 2, 4, H], F32))
        small = ps[:, 0, 0].rearrange("p k h -> p (k h)")

        setup = sem("setup")
        passed = sem("passed")
        turned = sem("turned")
        ready = sem("ready")
        link = sem("link")
        st_loaded = sem("st_loaded")
        root_ready = sem("root_ready")
        veps_ready = sem("veps_ready")
        scl_ready = sem("scl_ready")
        w2n_ready = sem("w2n_ready")
        mean_ready = sem("mean_ready")
        bias_ready = sem("bias_ready")
        xs_loaded, ys_loaded, ys_stored = sems("xs_loaded"), sems("ys_loaded"), sems("ys_stored")
        sums_ready = sems("sums_ready")
        gates_ready = sems("gates_ready")
        parts_ready = sems("parts_ready")
        cell_ready = sems("cell_ready")
        tanh_ready = sems("tanh_ready")
        hid_ready = sems("hid_ready")
        added = sems("added")
        block_done = sems("block_done")

        rows_of = [min(H, T * (tb + 1) + 1) for tb in range(BLOCKS)]
        per_half = 1 + (BLOCKS - 1) + STEPS

        def steps(eng, half_i, tb, body):
            eng.sem_inc(passed, 1)
            with eng.Fori(0, T // 2) as i:
                for par_ in range(2):
                    body(half_i * STEPS + (tb * T + 2 * i + par_), 2 * i + par_, par_)

        def groups_of(t, half_i, g):
            return t[bass.ds(half_i * (GH * GB) + GB * g, GB)]

        block = ctx.enter_context(nc.Block(name="lstm"))

        @block.sync
        def _(sp):
            for p in range(2):
                sp.sem_inc(ys_stored[p], 1)
            sp.dma_start(ident[:], const["ident"]).then_inc(setup, 16)
            sp.dma_start(w2raw[:], par["W2"]).then_inc(setup, 16)
            sp.dma_start(w1raw[:], par["W1"]).then_inc(setup, 16)
            sp.dma_start(b1row[:], par["b1"].rearrange("(k o) -> k o", k=4)).then_inc(setup, 16)
            sp.dma_start(b2row[:], par["b2"].rearrange("(k o) -> k o", k=4)).then_inc(setup, 16)

            with sp.Fori(0, 2) as hf:
                def load(tb):
                    p, n, t0 = tb % 2, rows_of[tb], T * tb
                    before = max(0, tb - 1)
                    for g in range(GH):
                        sp.wait_ge(sums_ready[g], hf * STEPS + T * before + 1)
                    sp.sem_inc(passed, 1)
                    for g in range(GH):
                        skewed = groups_of(src, hf, g).rearrange("b c h w -> (b c) (h w)")[:, PAD + t0:PAD + t0 + n * (WX - 1)]
                        sp.dma_start(xs[p][:, g, 0:n, :], skewed.rearrange("p (h w) -> p h w", w=WX - 1)[:, :, 0:T]).then_inc(xs_loaded[p], 16)
                    sp.wait_ge(ys_stored[p], (hf * (BLOCKS // 2) + tb // 2) * 32 + 1)
                    for g in range(GH):
                        cells = groups_of(src, hf, g).rearrange("b c h w -> (b c) h w")[:, :, PAD + t0:PAD + t0 + T]
                        sp.dma_start(ys[p][:, g], cells).then_inc(ys_loaded[p], 16)

                sp.wait_ge(bias_ready, hf + 1)
                sp.sem_inc(passed, 1)
                for g in range(GH):
                    sp.wait_ge(sums_ready[g], hf * STEPS + 1)
                    sp.dma_start(st[:, g], groups_of(stats, hf, g).rearrange("b c s -> (b c) s")).then_inc(st_loaded, 16)
                load(0)
                for tb in range(BLOCKS):
                    if tb + 1 < BLOCKS:
                        load(tb + 1)
                    for g in range(GH):
                        sp.wait_ge(block_done[g], hf * BLOCKS + tb + 2)
                        cells = groups_of(out, hf, g).rearrange("b c h w -> (b c) h w")[:, :, T * tb:T * (tb + 1)]
                        sp.dma_start(cells, ys[tb % 2][:, g]).then_inc(ys_stored[tb % 2], 16)
            for p in range(2):
                sp.wait_ge(ys_stored[p], BLOCKS * 32 + 1)

        @block.tensor
        def _(pe):
            for g in range(GH):
                pe.sem_inc(sums_ready[g], 1)
            pe.wait_ge(setup, 80)
            pe.wait_ge(link, 1)
            nc.tensor.transpose(small[0:C, 0:P], w2raw[:], ident[:])
            for j in range(2):
                nc.tensor.transpose(small[0:C, P * (1 + j):P * (2 + j)], w1raw[:, :, j], ident[:])
            nc.tensor.transpose(small[0:C, 3 * P:3 * P + 4], brow[:], ident[0:4, 0:4]).then_inc(turned, 1)
            pe.wait_ge(ready, 1)

            with pe.Fori(0, 2) as hf:
                pe.wait_ge(w2n_ready, hf + 1)
                for g in range(GH):
                    for k in range(4):
                        ins = nc.tensor.matmul(small[:, 4 * g + k:4 * g + k + 1], w2n[:, g, k], st[:, g, 0:1], start=True, stop=True)
                ins.then_inc(mean_ready, 1)
                pe.wait_ge(bias_ready, hf + 2)
                for tb in range(BLOCKS):
                    n, p = rows_of[tb], tb % 2
                    pe.wait_ge(xs_loaded[p], (hf * (BLOCKS // 2) + tb // 2 + 1) * 32)

                    def step(done, tau, par_):
                        for g in range(GH):
                            to = ps[:, g, par_]
                            pe.wait_ge(gates_ready[g], done + 1)
                            for k in range(4):
                                nc.tensor.matmul(to[:, k, 0:n], w2n[:, g, k], xs[p][:, g, 0:n, bass.ds(tau, 1)].rearrange("p h t -> p (h t)"),
                                                 start=k % 2 == 0, stop=False, skip_group_check=True)
                            pe.wait_ge(hid_ready[g], hf * (per_half - STEPS) + 1 + tb + done)
                            for k in range(4):
                                nc.tensor.matmul(to[:, k, 0:n], w1d[:, 0, k], hid[:, g, 0:n], start=False, stop=False, skip_group_check=True)
                                ins = nc.tensor.matmul(to[:, k, 0:n], w1d[:, 1, k], hid[:, g, 1:n + 1], start=False, stop=True,
                                                       skip_group_check=True)
                            ins.then_inc(sums_ready[g], 1)
                    steps(pe, hf, tb, step)

        @block.scalar
        def _(act):
            for g in range(GH):
                act.sem_inc(gates_ready[g], 2)
            with act.Fori(0, 2) as hf:
                act.wait_ge(veps_ready, hf + 1)
                nc.scalar.activation(root[:], veps[:], ACT.Sqrt).then_inc(root_ready, 1)
                act.wait_ge(bias_ready, hf + 2)
                for tb in range(BLOCKS):
                    n = rows_of[tb]

                    def step(done, tau, par_):
                        for g in range(GH):
                            act.wait_ge(sums_ready[g], done + 2)
                            for k in (FORGET, IN, CELL, OUT):
                                f = ACT.Tanh if k == CELL else ACT.Sigmoid
                                ins = nc.scalar.activation(gate[:, g, k, 0:n], ps[:, g, par_, k, 0:n], f, bias=bias[:, g, k:k + 1])
                            ins.then_inc(gates_ready[g], 1)
                            act.wait_ge(cell_ready[g], done + 1)
                            nc.scalar.activation(tc[:, g, 0:n], cell[:, g, 0:n], ACT.Tanh).then_inc(tanh_ready[g], 1)
                    steps(act, hf, tb, step)

        @block.vector
        def _(dve):
            v = nc.vector
            dve.sem_inc(bias_ready, 1)
            v.memset(w2d[:], 0.0)
            v.memset(w1d[:], 0.0)
            dve.wait_ge(setup, 80)
            v.tensor_tensor(brow[:], b1row[:], b2row[:], ALU.add).then_inc(link, 1)
            dve.wait_ge(link, 1)
            dve.wait_ge(turned, 1)
            for q in range(GB):
                here = slice(C * q, C * (q + 1))
                v.tensor_copy(w2d[here, :, here], small[0:C, 0:P].rearrange("p (k o) -> p k o", k=4))
                for j in range(2):
                    v.tensor_copy(w1d[here, j, :, here], small[0:C, P * (1 + j):P * (2 + j)].rearrange("p (k o) -> p k o", k=4))
                ins = v.tensor_copy(b12[here, :], small[0:C, 3 * P:3 * P + 4])
            ins.then_inc(ready, 1)
            dve.wait_ge(ready, 1)

            with dve.Fori(0, 2) as hf:
                c = Count(hf * 5 + 1)

                def chained(ins):
                    ins.then_inc(link, 1)
                    dve.wait_ge(link, c.next())

                dve.wait_ge(st_loaded, hf * 32 + 32)
                chained(v.tensor_scalar(veps[:], st[:, :, 1], EPS, None, ALU.add))
                dve.sem_inc(veps_ready, 1)
                dve.wait_ge(root_ready, hf + 1)
                chained(v.reciprocal(inv[:], root[:]))
                chained(v.tensor_tensor(half[:], inv[:], inv[:], ALU.mult))
                chained(v.tensor_tensor(half[:], half[:], veps[:], ALU.mult))
                chained(v.tensor_scalar(half[:], half[:], -0.5, 1.5, ALU.mult, ALU.add))
                v.tensor_tensor(scl[:], inv[:], half[:], ALU.mult).then_inc(scl_ready, 1)
                dve.wait_ge(scl_ready, hf + 1)
                for g in range(GH):
                    ins = v.tensor_scalar(w2n[:, g], w2d[:], scl[:, g:g + 1], None, ALU.mult)
                ins.then_inc(w2n_ready, 1)
                dve.wait_ge(mean_ready, hf + 1)
                for g in range(GH):
                    ins = v.tensor_tensor(bias[:, g], b12[:], small[:, 4 * g:4 * g + 4], ALU.subtract)
                ins.then_inc(bias_ready, 1)
                for g in range(GH):
                    dve.wait_ge(added[g], hf * STEPS + 1)
                    v.memset(cell[:, g], 0.0)
                    v.memset(hid[:, g], 0.0).then_inc(hid_ready[g], 1)
                for tb in range(BLOCKS):
                    n = rows_of[tb]
                    if tb:
                        m = rows_of[tb - 1]
                        for g in range(GH):
                            dve.wait_ge(hid_ready[g], hf * per_half + tb + T * tb)
                            v.tensor_copy(cell[:, g, m:n], cell[:, g, m - 1:m].broadcast_to([P, n - m]))
                            v.tensor_copy(hid[:, g, m + 1:n + 1], hid[:, g, m:m + 1].broadcast_to([P, n - m])).then_inc(hid_ready[g], 1)
                            dve.wait_ge(hid_ready[g], hf * per_half + tb + T * tb + 1)
                    else:
                        for g in range(GH):
                            dve.wait_ge(hid_ready[g], hf * per_half + 1)

                    def step(done, tau, par_):
                        for g in range(GH):
                            dve.wait_ge(gates_ready[g], done + 3)
                            v.tensor_tensor(fc[:, g, 0:n], gate[:, g, FORGET, 0:n], cell[:, g, 0:n], ALU.mult)
                            v.tensor_tensor(ig[:, g, 0:n], gate[:, g, IN, 0:n], gate[:, g, CELL, 0:n], ALU.mult).then_inc(parts_ready[g], 1)
                            dve.wait_ge(parts_ready[g], done + 1)
                            v.tensor_tensor(cell[:, g, 0:n], fc[:, g, 0:n], ig[:, g, 0:n], ALU.add).then_inc(cell_ready[g], 1)
                            dve.wait_ge(tanh_ready[g], done + 1)
                            dve.wait_ge(added[g], done + 1)
                            v.tensor_tensor(hid[:, g, 1:n + 1], gate[:, g, OUT, 0:n], tc[:, g, 0:n], ALU.mult).then_inc(hid_ready[g], 1)
                    steps(dve, hf, tb, step)

        @block.gpsimd
        def _(pl):
            v = nc.gpsimd
            for g in range(GH):
                pl.sem_inc(added[g], 1)
                pl.sem_inc(block_done[g], 1)
            with pl.Fori(0, 2) as hf:
                for tb in range(BLOCKS):
                    n, p = rows_of[tb], tb % 2
                    pl.wait_ge(ys_loaded[p], (hf * (BLOCKS // 2) + tb // 2 + 1) * 32)
                    for g in range(GH):
                        pl.wait_ge(block_done[g], hf * BLOCKS + tb + 1)

                    def step(done, tau, par_):
                        for g in range(GH):
                            pl.wait_ge(hid_ready[g], hf * (per_half - STEPS) + 2 + tb + done)
                            if n < H:
                                v.tensor_copy(below[:, g, bass.ds(tau, 1)], hid[:, g, n:n + 1])
                            cells = ys[p][:, g, 0:n, bass.ds(tau, 1)].rearrange("p h t -> p (h t)")
                            v.tensor_tensor(cells, cells, hid[:, g, 1:n + 1], ALU.add).then_inc(added[g], 1)
                    steps(pl, hf, tb, step)
                    for g in range(GH):
                        pl.wait_ge(added[g], hf * STEPS + T * (tb + 1) + 1)
                        if n < H:
                            cells = ys[p][:, g, n:H, :]
                            v.tensor_tensor(cells, cells, below[:, g].unsqueeze(1).broadcast_to([P, H - n, T]), ALU.add).then_inc(block_done[g], 1)
                        else:
                            pl.sem_inc(block_done[g], 1)


def program(nc, x, const, out):
    x1 = nc.dram_tensor("x1", (NB, C, H, W), F32).ap()
    x3 = nc.dram_tensor("x3", (NB, C, H, WX), F32).ap()
    stats1 = nc.dram_tensor("stats1", (NB, C, 2), F32).ap()
    stats3 = nc.dram_tensor("stats3", (NB, C, 2), F32).ap()
    spectra = nc.dram_tensor("spectra", (NB, 2 * C, MM), F32).ap()
    mixed = nc.dram_tensor("mixed", (NB, 2 * C, MM), F32).ap()
    conv_phase(nc, 0, x["x"], x1, stats1, None, const, {"w": x["L0_conv_weight"]})
    spectrum_phase(nc, x1, spectra, const)
    mixing_phase(nc, spectra, stats1, x["L1_conv_weights1"], mixed)
    conv_phase(nc, 2, x1, x3, stats3, mixed, const,
               {"w1": x["L2_conv_w1"], "b1": x["L2_conv_b1"], "w2": x["L2_conv_w2"], "b2": x["L2_conv_b2"]})
    lstm_phase(nc, x3, out, stats3,
               {"W2": x["L3_conv_W2"], "W1": x["L3_conv_W1"], "b1": x["L3_conv_b1"], "b2": x["L3_conv_b2"]}, const)


def constants():
    import numpy as np
    p = np.arange(P)
    f = np.float64
    k = np.arange(M)
    ang_h = 2 * np.pi * np.outer(np.arange(H), k) / H
    ang_w = 2 * np.pi * np.outer(np.arange(W), k) / W
    i3 = np.zeros((P, 3, 2, C))
    for i in range(2):
        i3[C * (i + 1):C * (i + 2), 1, i, :] = np.eye(C)
    fh = np.concatenate([np.cos(ang_h), -np.sin(ang_h)], 1).reshape(2, P, 2 * M).transpose(1, 0, 2)
    fw = np.stack([np.concatenate([np.cos(ang_w), -np.sin(ang_w)], 1),
                   np.concatenate([np.sin(ang_w), np.cos(ang_w)], 1)], 1).reshape(2, P, 2, 2 * M).transpose(1, 0, 2, 3)
    eh = np.zeros((2 * C, H))
    eh[0:M] = np.cos(ang_h).T
    eh[C:C + M] = np.sin(ang_h).T
    twice = np.where(k == 0, 1.0, 2.0)[:, None] / (H * W)
    ew = np.concatenate([twice * np.cos(ang_w).T, -twice * np.sin(ang_w).T], 0)
    t = {
        "ident": np.eye(P),
        "g8": ((p[:, None] % C) // 2 == (p[None, :] % C) // 2) / 8.0,
        "g4": (p[:, None] % C == p[None, :] % C) / 4.0,
        "i3": i3.reshape(P, -1),
        "i4": (p[:, None] % C == np.arange(C)[None, :]) * 1.0,
        "ones": np.ones((P, PAD)),
        "fh": fh.reshape(P, -1), "fw": fw.reshape(P, -1), "eh": eh, "ew": ew,
    }
    return {n: np.ascontiguousarray(a, dtype=np.float32) for n, a in t.items()}


_INS = ['x', 'L0_conv_weight', 'L1_conv_weights1', 'L1_conv_weights2', 'L2_conv_w1', 'L2_conv_b1', 'L2_conv_w2',
        'L2_conv_b2', 'L3_conv_W2', 'L3_conv_b2', 'L3_conv_W1', 'L3_conv_b1']


def kernel(**inputs):
    import numpy as _np
    import concourse.bacc as _bacc
    from concourse import mybir as _mybir
    from concourse.bass_utils import run_bass_kernel_spmd as _run

    nc = _bacc.Bacc("TRN2", target_bir_lowering=False, num_devices=1)
    arrays, args, const = {}, {}, {}
    for name in _INS:
        a = _np.ascontiguousarray(inputs[name])
        arrays[f"in_{name}_dram"] = a
        args[name] = nc.dram_tensor(f"in_{name}_dram", a.shape, _mybir.dt.from_np(a.dtype), kind="ExternalInput").ap()
    for name, a in constants().items():
        arrays[f"const_{name}_dram"] = a
        const[name] = nc.dram_tensor(f"const_{name}_dram", a.shape, _mybir.dt.from_np(a.dtype), kind="ExternalInput").ap()
    out = nc.dram_tensor("out_0_dram", (NB, C, H, W), F32, kind="ExternalOutput").ap()
    program(nc, args, const, out)
    r = _run(nc, [arrays], core_ids=[0])
    return r.results[0]["out_0_dram"]
```

```python
from contextlib import ExitStack

import concourse.bass as bass
from concourse import mybir

F32 = mybir.dt.float32
ALU = mybir.AluOpType
ACT = mybir.ActivationFunctionType

NB, C, H, W = 16, 32, 256, 256
P = 128
S = P // C
KB = H // S
WP = W + 2
CK = 8
NCH = KB // CK
GK = 2
NG = CK // GK
NGI = NCH * NG
M = 16
MM = M * M
T = 16
PAD = 16
WX = PAD + W
EPS = 1e-5


DIV = float((C * 9) ** 0.5)
HC = 2 * NCH
HB = CK // 2


class Count:

    def __init__(self, base):
        self.base, self.n = base, 0

    def next(self):
        self.n += 1
        return self.base + self.n


def image_loop(eng, body):
    with eng.Fori(0, NB // 2 - 1) as i:
        for u in range(2):
            body(i * 2 + u, u, False, False)
    body(NB - 2, 0, False, True)
    body(NB - 1, 1, True, True)


def image(t, n):
    return t[bass.ds(n, 1)]


def conv_phase(nc, layer, src, dst, stats, spectra, const, par):
    second = layer == 2
    left = PAD if second else 0
    with ExitStack() as ctx:
        def sb(name, shape):
            return ctx.enter_context(nc.sbuf_tensor(f"{name}_l{layer}", shape, F32))

        def sem(name):
            return ctx.enter_context(nc.semaphore(f"{name}_l{layer}"))

        xa = [sb(f"xa{u}", [P, KB + 1, WP]) for u in range(2)]
        xb = [sb(f"xb{u}", [P, HB, WP]) for u in range(4)]
        xt = [sb(f"xt{u}", [P, WP]) for u in range(2)]
        oc = [sb(f"oc{u}", [P, HB, W]) for u in range(4)]
        ist = sb("ist", [P, NGI, 6])
        ost = sb("ost", [P, NGI, 6])
        agg_i = sb("agg_i", [P, 2])
        agg_o = sb("agg_o", [P, 2])
        grp_i = sb("grp_i", [P, 2])
        grp_o = sb("grp_o", [P, 2])
        scl = sb("scl", [P, 1])
        veps, root, inv, half = (sb(x, [P, 1]) for x in ("veps", "root", "inv", "half"))
        dev = sb("dev", [P, 1])
        var = sb("var", [P, 1])
        wn = sb("wn", [P, 3, 2, C])
        wf = [sb(f"wf{u}", [P, 3, 2, C]) for u in range(2)]
        nb = [sb(f"nb{u}", [P, 1]) for u in range(2)]
        ones = sb("ones", [P, WP])
        g8 = sb("g8", [P, P])
        i3 = sb("i3", [P, 3, 2, C])
        if not second:
            wraw = sb("wraw", [C, C, 3, 3])
            ident = sb("ident", [C, C])
            wb = sb("wb", [P, 3, 2, C])
        else:
            ident = sb("ident", [2 * C, 2 * C])
            g4 = sb("g4", [P, P])
            i4 = sb("i4", [P, C])
            w1 = sb("w1", [C, P])
            b1 = sb("b1", [P, 1])
            w2raw = sb("w2raw", [P, C, 3, 3])
            w2r = sb("w2r", [P, 3, 2, S, C])
            b2c = sb("b2c", [C, 3, 3])
            b2r = sb("b2r", [P, 3, 2])
            pool = sb("pool", [P, 1])
            hdn = sb("hdn", [P, 1])
            kern = sb("kern", [P, 6])
            kn = sb("kn", [P, 6])
            mpad = sb("mpad", [P, PAD])
            mpads = sb("mpads", [P, KB, PAD])
            o1 = [sb(f"o1{u}", [2 * C, M, M]) for u in range(2)]
            tt = sb("tt", [2 * C, C, 2, M])
            eh = sb("eh", [2 * C, H])
            ew = sb("ew", [C, W])
            gs = sb("gs", [C, H // 2, C])

        cps = ctx.enter_context(nc.psum_tensor(f"cps_l{layer}", [P, 4, GK, W], F32))
        yps = ctx.enter_context(nc.psum_tensor(f"yps_l{layer}", [P, 3, GK, W], F32))
        sm = ctx.enter_context(nc.psum_tensor(f"sm_l{layer}", [P, 512], F32))

        passed = sem("passed")
        setup = sem("setup")
        turned = sem("turned")
        ready = sem("ready")
        xa_loaded = [[sem(f"xa_loaded{u}_{j}") for j in range(NCH // 2)] for u in range(2)]
        xa_final = sem("xa_final")
        taps_ready = sem("taps_ready")
        xb_loaded = [sem(f"xb_loaded{u}") for u in range(4)]
        xt_loaded = [sem(f"xt_loaded{u}") for u in range(2)]
        conv_ready = sem("conv_ready")
        evac = sem("evac")
        ostat = sem("ostat")
        istat = sem("istat")
        stored = [sem(f"stored{u}") for u in range(4)]
        link = sem("link")
        v2p = sem("v2p")
        p2v = sem("p2v")
        var_ready = sem("var_ready")
        root_ready = sem("root_ready")
        nb_ready = sem("nb_ready")
        grp_ready = sem("grp_ready")
        grp_stored = sem("grp_stored")
        o1_loaded = [sem(f"o1_loaded{u}") for u in range(2)]
        t_ready = sem("t_ready")
        t_copied = sem("t_copied")
        g_ready = sem("g_ready")
        g_copied = sem("g_copied")
        y_ready = sem("y_ready")
        y_added = sem("y_added")

        K_IN = 5 if second else 3
        K = K_IN + 2
        N_SETUP = 16 * (12 if second else 4)
        banks_of = [0] * 3 + [4] * 4 + [0] * 2 + [4] * 4 + [0] * 3 if second else [4] * 8 + [0] * 8
        spectra_at = {(1, 0): (0, 0), (1, 1): (0, 2), (2, 0): (0, 4), (2, 1): (0, 6),
                      (7, 1): (1, 0), (8, 0): (1, 2), (8, 1): (1, 4), (9, 0): (1, 6)} if second else {}
        starts = [sum(banks_of[:h]) for h in range(HC)]

        def load_chunk(eng, n, u, j):
            for s in range(S):
                rows = image(src, n).rearrange("b c (k s) w -> s (b c) k w", s=S)[s][:, CK * j:CK * (j + 1)]
                eng.dma_start(xa[u][C * s:C * (s + 1), CK * j:CK * (j + 1), 1:W + 1], rows).then_inc(xa_loaded[u][j // 2], 16)

        block = ctx.enter_context(nc.Block(name=f"conv{layer}"))

        @block.sync
        def _(sp):
            for o in range(4):
                sp.sem_inc(stored[o], 1)
            sp.sem_inc(grp_stored, 16 * (1 + S * second) + 1)
            for u in range(2):
                for j in range(NCH):
                    load_chunk(sp, u, u, j)

            def body(n, u, last, tail):
                for h in range(HC):
                    sp.wait_ge(evac, n * NGI + 4 + 2 * (h + 1))
                    o = h % 4
                    for s in range(S):
                        blocks = HB - (h == HC - 1 and s == S - 1)
                        r0 = h * HB * S + 1 + s
                        rows = image(dst, n)[:, :, r0:r0 + (blocks - 1) * S + 1:S, left:left + W]
                        sp.dma_start(rows.rearrange("b c k w -> (b c) k w"),
                                     oc[o][C * s:C * (s + 1), 0:blocks, :]).then_inc(stored[o], 16)
                    if h == HC - 1:
                        row = image(dst, n)[:, :, 0:1, left:left + W]
                        sp.dma_start(row.rearrange("b c k w -> (b c) k w"),
                                     oc[o][3 * C:P, HB - 1:HB, :]).then_inc(stored[o], 16)
                    if h % 2 == 1 and not tail:
                        load_chunk(sp, n + 2, u, h // 2)
                sp.wait_ge(grp_ready, n + 2)
                sp.dma_start(image(stats, n).rearrange("b c s -> (b c) s"), grp_o[0:C, :]).then_inc(grp_stored, 16)
                if second:
                    for s in range(S):
                        cells = image(dst, n).rearrange("b c (k s) w -> s (b c) k w", s=S)[s][:, :, 0:PAD]
                        sp.dma_start(cells, mpads[C * s:C * (s + 1)]).then_inc(grp_stored, 16)

            image_loop(sp, body)
            for o in range(4):
                sp.wait_ge(stored[o], NB * 16 * (4 * S + (o == 3)) + 1)
            sp.wait_ge(grp_stored, (NB + 1) * 16 * (1 + S * second) + 1)

        @block.gpsimd
        def _(pl):
            if second:
                for u in range(2):
                    pl.dma_start(o1[u][:], spectra[u].rearrange("p (x y) -> p x y", y=M)).then_inc(o1_loaded[u], 16)

            def body(n, u, last, tail):
                if second and not tail:
                    pl.wait_ge(t_ready, n + 1)
                    pl.sem_inc(passed, 1)
                    pl.dma_start(o1[u][:], image(spectra, n + 2).rearrange("b p (x y) -> (b p) x y", y=M)).then_inc(o1_loaded[u], 16)
                pl.wait_ge(xa_final, n + 1)
                pl.sem_inc(passed, 1)
                pl.dma_start(xt[u][2 * C:P, :], xa[u][0:2 * C, 0, :]).then_inc(xt_loaded[u], 16)
                for h in range(HC):
                    pl.wait_ge(conv_ready, n * NGI + 2 * h + 2)
                    pl.sem_inc(passed, 1)
                    k = HB * h
                    pl.dma_start(xb[h % 4][0:2 * C], xa[u][2 * C:P, k:k + HB, :]).then_inc(xb_loaded[h % 4], 16)
                    pl.dma_start(xb[h % 4][2 * C:P], xa[u][0:2 * C, k + 1:k + HB + 1, :]).then_inc(xb_loaded[h % 4], 16)
            image_loop(pl, body)

        @block.tensor
        def _(pe):
            def input_mean(c):
                pe.wait_ge(v2p, c.next())
                if second:
                    nc.tensor.matmul(sm[:, 2:3], g4[:], agg_i[:, 0:1], start=True, stop=True)
                nc.tensor.matmul(sm[:, 0:1], g8[:], agg_i[:, 0:1], start=True, stop=True).then_inc(p2v, 1)

            def output_mean(c):
                pe.wait_ge(v2p, c.next())
                nc.tensor.matmul(sm[:, 0:1], g8[:], agg_o[:, 0:1], start=True, stop=True).then_inc(p2v, 1)

            def variance(c):
                pe.wait_ge(v2p, c.next())
                nc.tensor.matmul(sm[:, 1:2], g8[:], var[:], start=True, stop=True).then_inc(p2v, 1)

            def hidden(c):
                pe.wait_ge(v2p, c.next())
                nc.tensor.matmul(sm[:, 3:4], w1[:], pool[0:C, :], start=True, stop=True).then_inc(p2v, 1)

            def predicted(c):
                pe.wait_ge(v2p, c.next())
                for t in range(6):
                    ins = nc.tensor.matmul(sm[:, 4 + t:5 + t], w2r[:, t // 2, t % 2], hdn[:], start=True, stop=True)
                ins.then_inc(p2v, 1)

            def bias(c):
                pe.wait_ge(v2p, c.next())
                for t in range(2):
                    for dw in range(3):
                        ins = nc.tensor.matmul(sm[2 * C * t:2 * C * (t + 1), 10:11], wn[:, dw], grp_i[:, 0:1],
                                               start=dw == 0, stop=dw == 2)
                ins.then_inc(p2v, 1)

            def conv_bank(n, u, h, g):
                b = (2 * h + g) % 4
                pe.wait_ge(evac, n * NGI + 2 * h + g + 1)
                k = HB * h + GK * g
                end = h == HC - 1 and g == 1
                copy_b = xb[h % 4][:, GK * g:GK * (g + 1)]
                for dw in range(3):
                    f = dict(start=dw == 0, stop=dw == 2)
                    ins = nc.tensor.matmul(cps[0:2 * C, b], wf[u][:, dw], xa[u][:, k:k + GK, dw:dw + W], **f)
                    if not end:
                        ins = nc.tensor.matmul(cps[2 * C:P, b], wf[u][:, dw], copy_b[:, :, dw:dw + W], **f)
                if end:
                    for dw in range(3):
                        nc.tensor.matmul(cps[2 * C:P, b, 0], wf[u][:, dw], copy_b[:, 0, dw:dw + W],
                                         start=dw == 0, stop=dw == 2)
                    for dw in range(3):
                        nc.tensor.matmul(cps[2 * C:3 * C, b, 1], wf[u][:, dw, 0], copy_b[:, 1, dw:dw + W],
                                         start=dw == 0, stop=dw == 2)
                    for dw in range(3):
                        ins = nc.tensor.matmul(cps[3 * C:P, b, 1], wf[u][:, dw, 1], xt[u][:, dw:dw + W],
                                               start=dw == 0, stop=dw == 2)
                ins.then_inc(conv_ready, 1)

            def turn_modes(n, u):
                pe.wait_ge(o1_loaded[u], (n - u) * 8 + 16)
                pe.wait_ge(y_added, n * NGI + 1)
                pe.sem_inc(passed, 1)
                for ky in range(M):
                    bank = yps[0:M, ky // 8].rearrange("p a b -> p (a b)")
                    ins = nc.tensor.transpose(bank[:, 64 * (ky % 8):64 * (ky % 8) + 64], o1[u][:, :, ky], ident[:])
                ins.then_inc(t_ready, 1)

            def row_spectra(n, half, q0):
                for q in range(q0, q0 + 2):
                    if q == 0:
                        pe.wait_ge(t_copied, n + 1)
                        pe.wait_ge(y_added, n * NGI + half * NGI // 2 + 1)
                    if q >= 3:
                        pe.wait_ge(g_copied, n * 16 + half * 8 + q - 2)
                    nc.tensor.matmul(yps[:, q % 3, 0, 0:H // 2], tt[:, 4 * q:4 * q + 4], eh[:, half * H // 2:(half + 1) * H // 2],
                                     start=True, stop=True).then_inc(g_ready, 1)

            def inverse_bank(n, g):
                if g % (NGI // 2) == 0:
                    pe.wait_ge(g_copied, n * 16 + 8 * (g // (NGI // 2)) + 8)
                if g >= 3:
                    pe.wait_ge(y_added, n * NGI + g - 1)
                for r in range(GK):
                    row = (GK * g + r) * S % (H // 2)
                    ins = nc.tensor.matmul(yps[:, g % 3, r], gs[:, row:row + S], ew[:], start=True, stop=True)
                ins.then_inc(y_ready, 1)

            pe.sem_inc(conv_ready, 8)
            pe.wait_ge(setup, N_SETUP)
            if not second:
                for t in range(9):
                    ins = nc.tensor.transpose(sm[0:C, C * t:C * (t + 1)], wraw[:, :, t // 3, t % 3], ident[:])
                ins.then_inc(turned, 1)
            pe.wait_ge(ready, 1)
            if second:
                turn_modes(0, 0)
                for half in range(2):
                    for q in range(0, 8, 2):
                        row_spectra(0, half, q)
                    for g in range(NGI // 2):
                        inverse_bank(0, NGI // 2 * half + g)
                turn_modes(1, 1)
            c = Count(0)
            input_mean(c)
            variance(c)
            if second:
                hidden(c)
                predicted(c)
            bias(c)

            def body(n, u, last, tail):
                c = Count(K_IN + n * K)
                for h in range(HC):
                    if h == 0:
                        pe.wait_ge(taps_ready, n + 1)
                        pe.wait_ge(xt_loaded[u], (n - u) * 8 + 16)
                    pe.wait_ge(xb_loaded[h % 4], n * 128 + (h // 4 + 1) * 32)
                    if second and not tail and h == 14:
                        turn_modes(n + 2, u)
                    for g in range(2):
                        if not last and (h, g) in spectra_at:
                            row_spectra(n + 1, *spectra_at[h, g])
                        conv_bank(n, u, h, g)
                        if (h, g) == (0, 1):
                            output_mean(c)
                        if (h, g) == (1, 0):
                            variance(c)
                        if last:
                            continue
                        if second:
                            for gg in range(banks_of[h] // 2):
                                inverse_bank(n + 1, starts[h] + banks_of[h] // 2 * g + gg)
                        if (h, g) == (13, 0):
                            input_mean(c)
                        if (h, g) == (13, 1):
                            variance(c)
                        if (h, g) == (14, 0) and second:
                            hidden(c)
                        if (h, g) == (14, 1) and second:
                            predicted(c)
                        if (h, g) == ((15, 0) if second else (14, 0)):
                            bias(c)
            image_loop(pe, body)
            c = Count(K_IN + (NB - 1) * K + 2)
            output_mean(c)
            variance(c)

        @block.scalar
        def _(act):
            def copy_modes(n):
                act.wait_ge(t_ready, n + 1)
                for b in range(2):
                    v = yps[0:M, b].rearrange("p a b -> p (a b)").rearrange("p (y r o) -> p r o y", r=2, o=C)
                    y = slice(8 * b, 8 * b + 8)
                    for r in range(2):
                        nc.scalar.activation(tt[0:M, :, r, y], v[:, r], ACT.Copy)
                    nc.scalar.activation(tt[C:C + M, :, 0, y], v[:, 1], ACT.Copy, scale=-1.0)
                    ins = nc.scalar.activation(tt[C:C + M, :, 1, y], v[:, 0], ACT.Copy)
                ins.then_inc(t_copied, 1)

            def copy_spectra(n, half, q0):
                for q in range(q0, q0 + 2):
                    act.wait_ge(g_ready, n * 16 + half * 8 + q + 1)
                    for o in range(4):
                        ins = nc.scalar.activation(gs[:, :, 4 * q + o], yps[C * o:C * (o + 1), q % 3, 0, 0:H // 2], ACT.Copy)
                    ins.then_inc(g_copied, 1)

            def root_of(n):
                act.wait_ge(var_ready, n + 1)
                nc.scalar.activation(root[:], veps[:], ACT.Sqrt).then_inc(root_ready, 1)

            act.dma_start(g8[:], const["g8"]).then_inc(setup, 16)
            act.dma_start(i3[:], const["i3"].rearrange("p (a b c) -> p a b c", a=3, b=2)).then_inc(setup, 16)
            n_id = 2 * C if second else C
            act.dma_start(ident[:], const["ident"][0:n_id, 0:n_id]).then_inc(setup, 16)
            if not second:
                act.dma_start(wraw[:], par["w"]).then_inc(setup, 16)
            else:
                act.dma_start(g4[:], const["g4"]).then_inc(setup, 16)
                act.dma_start(i4[:], const["i4"]).then_inc(setup, 16)
                act.dma_start(eh[:], const["eh"]).then_inc(setup, 16)
                act.dma_start(ew[:], const["ew"]).then_inc(setup, 16)
                act.dma_start(w1[:], par["w1"]).then_inc(setup, 16)
                act.dma_start(b1[:], par["b1"].rearrange("(a b) -> a b", b=1)).then_inc(setup, 16)
                act.dma_start(w2raw[:], par["w2"].rearrange("p (c h w) -> p c h w", h=3, w=3)).then_inc(setup, 16)
                act.dma_start(mpad[:], const["ones"][:, 0:PAD]).then_inc(setup, 16)
                act.dma_start(b2c[:], par["b2"].rearrange("(c h w) -> c h w", h=3, w=3)).then_inc(setup, 16)
            act.sem_inc(evac, 4)
            act.wait_ge(ready, 1)
            if second:
                copy_modes(0)
                for half in range(2):
                    for q in range(0, 8, 2):
                        copy_spectra(0, half, q)
                copy_modes(1)
            root_of(0)

            def body(n, u, last, tail):
                act.wait_ge(nb_ready, n + 1)
                for h in range(HC):
                    o = h % 4
                    act.wait_ge(stored[o], n * 16 * (4 * S + (o == 3)) + 16 * S * (h // 4) + 1)
                    act.wait_ge(ostat, n * HC + h + 1)
                    if second and not tail and h == 14:
                        copy_modes(n + 2)
                    for g in range(2):
                        if not last and (h, g) in spectra_at:
                            copy_spectra(n + 1, *spectra_at[h, g])
                        act.wait_ge(conv_ready, n * NGI + 8 + 2 * h + g + 1)
                        nc.scalar.activation(oc[o][:, GK * g:GK * (g + 1)], cps[:, (2 * h + g) % 4], ACT.Identity,
                                             bias=nb[u][:, 0:1]).then_inc(evac, 1)
                    if h == 13 and not last:
                        root_of(n + 1)
            image_loop(act, body)

        @block.vector
        def _(dve):
            v = nc.vector

            def chained(c, ins):
                ins.then_inc(link, 1)
                dve.wait_ge(link, c.next())

            c = Count(0)
            dve.sem_inc(ostat, 4)
            dve.sem_inc(y_added, 1)
            v.memset(ones[:], 1.0)
            v.memset(ost[:], 1.0)
            for u in range(2):
                v.memset(xa[u][2 * C:P, KB, :], 0.0)
            if not second:
                chained(c, v.memset(wb[:], 0.0))
                dve.wait_ge(turned, 1)
                w = sm[0:C, 0:9 * C].rearrange("p (h w o) -> p h w o", h=3, w=3)
                for i in range(2):
                    for kh in range(3):
                        j = i + kh
                        ins = v.tensor_scalar(wb[C * j:C * (j + 1), :, i, :], w[:, kh], 0.0, 2.0 / DIV, ALU.is_gt, ALU.mult)
                chained(c, ins)
                for i in range(2):
                    for kh in range(3):
                        j = i + kh
                        cells = wb[C * j:C * (j + 1), :, i, :]
                        ins = v.tensor_scalar(cells, cells, -1.0 / DIV, None, ALU.add)
                chained(c, ins)
            else:
                v.memset(b2r[:], 0.0)
                v.memset(tt[:], 0.0)
                chained(c, v.memset(w2r[:], 0.0))
                dve.wait_ge(setup, N_SETUP)
                for i in range(2):
                    for kh in range(3):
                        for kw in range(3):
                            v.tensor_copy(w2r[:, kw, i, i + kh, :], w2raw[:, :, kh, kw])
                        j = i + kh
                        ins = v.tensor_copy(b2r[C * j:C * (j + 1), :, i], b2c[:, kh, :])
                chained(c, ins)
            dve.sem_inc(ready, 1)
            dve.wait_ge(setup, N_SETUP)

            def input_banks(n, u, g0, g1):
                for g in range(g0, g1):
                    cells = xa[u][:, GK * g:GK * (g + 1), 1:W + 1]
                    if g % (2 * NG) == 0:
                        dve.wait_ge(xa_loaded[u][g // (2 * NG)], (n - u) * 64 + 128)
                    if second:
                        dve.wait_ge(y_ready, n * NGI + g + 1)
                        v.tensor_tensor(cells, cells, yps[:, g % 3], ALU.add).then_inc(y_added, 1)
                        dve.wait_ge(y_added, n * NGI + g + 2)
                    ins = v.bn_stats(ist[:, g, :], cells)
                    if g == NGI - 1:
                        ins.then_inc(istat, 1)

            def mean(c, cp, agg, st, grp):
                v.bn_aggr(agg[:], st[:].rearrange("p g s -> p (g s)")).then_inc(v2p, 1)
                dve.wait_ge(p2v, cp.next())
                v.tensor_copy(grp[:, 0:1], sm[:, 0:1])
                chained(c, v.tensor_tensor(dev[:], agg[:, 0:1], sm[:, 0:1], ALU.subtract))
                v.scalar_tensor_tensor(out=var[:], in0=dev[:], scalar=dev[:, 0:1], in1=agg[:, 1:2],
                                       op0=ALU.mult, op1=ALU.add).then_inc(v2p, 1)

            def input_norm(c, cp, n, u):
                dve.wait_ge(istat, n + 1)
                dve.sem_inc(passed, 1)
                mean(c, cp, agg_i, ist, grp_i)
                v.tensor_scalar(xa[u][:, 0:KB, 0:W + 2:W + 1], ones[:, 0:2 * KB].rearrange("p (a b) -> p a b", b=2),
                                grp_i[:, 0:1], None, ALU.mult)
                v.tensor_scalar(xt[u][0:2 * C, :], ones[0:2 * C, :], grp_i[0:2 * C, 0:1], None, ALU.mult)
                v.tensor_scalar(xa[u][0:2 * C, KB, :], ones[0:2 * C, :], grp_i[0:2 * C, 0:1], None,
                                ALU.mult).then_inc(xa_final, 1)
                dve.wait_ge(p2v, cp.next())
                chained(c, v.tensor_scalar(veps[:], sm[:, 1:2], EPS, None, ALU.add))
                dve.sem_inc(var_ready, 1)
                dve.wait_ge(root_ready, n + 1)
                chained(c, v.reciprocal(inv[:], root[:]))
                chained(c, v.scalar_tensor_tensor(out=half[:], in0=inv[:], scalar=inv[:, 0:1], in1=veps[:],
                                                  op0=ALU.mult, op1=ALU.mult))
                chained(c, v.tensor_scalar(half[:], half[:], -0.5, 1.5, ALU.mult, ALU.add))
                chained(c, v.tensor_tensor(scl[:], inv[:], half[:], ALU.mult))
                if second:
                    v.tensor_scalar(pool[:], sm[:, 2:3], grp_i[:, 0:1], scl[:, 0:1], ALU.subtract, ALU.mult).then_inc(v2p, 1)
                else:
                    v.tensor_scalar(wn[:], wb[:], scl[:, 0:1], None, ALU.mult).then_inc(v2p, 1)

            def predict(c, cp):
                dve.wait_ge(p2v, cp.next())
                v.tensor_scalar(hdn[:], sm[:, 3:4], b1[:, 0:1], 0.0, ALU.add, ALU.max).then_inc(v2p, 1)
                dve.wait_ge(p2v, cp.next())
                chained(c, v.tensor_tensor(kern[:], sm[:, 4:10], b2r[:].rearrange("p a b -> p (a b)"), ALU.add))
                chained(c, v.tensor_scalar(kn[:], kern[:], scl[:, 0:1], None, ALU.mult))
                taps6 = wn[:].rearrange("p a b o -> p (a b) o")
                for t in range(6):
                    ins = v.tensor_scalar(taps6[:, t, :], i4[:], kn[:, t:t + 1], None, ALU.mult)
                ins.then_inc(v2p, 1)

            def taps(cp, u):
                dve.wait_ge(p2v, cp.next())
                v.tensor_tensor(wf[u][:], wn[:], i3[:], ALU.add).then_inc(taps_ready, 1)
                v.tensor_scalar(nb[u][:], sm[:, 10:11], -1.0, None, ALU.mult).then_inc(nb_ready, 1)

            def output_norm(c, cp, n):
                dve.wait_ge(ostat, n * HC + 4)
                dve.wait_ge(grp_stored, n * 16 * (1 + S * second) + 1)
                dve.sem_inc(passed, 1)
                mean(c, cp, agg_o, ost, grp_o)
                dve.wait_ge(p2v, cp.next())
                chained(c, v.tensor_copy(grp_o[:, 1:2], sm[:, 1:2]))
                if second:
                    v.tensor_scalar(mpads[:], mpad[:].unsqueeze(1).broadcast_to([P, KB, PAD]), grp_o[:, 0:1],
                                    None, ALU.mult).then_inc(grp_ready, 1)
                else:
                    dve.sem_inc(grp_ready, 1)

            input_banks(0, 0, 0, NGI)
            cp = Count(0)
            input_norm(c, cp, 0, 0)
            if second:
                predict(c, cp)
            taps(cp, 0)
            c0 = c.n
            links = 10 if second else 8

            def body(n, u, last, tail):
                c, cp = Count(c0 + n * links), Count(K_IN + n * K)
                output_norm(c, cp, n)
                for h in range(HC):
                    if not last:
                        input_banks(n + 1, 1 - u, starts[h], starts[h] + banks_of[h])
                        if h == 13:
                            input_norm(c, cp, n + 1, 1 - u)
                        if h == 14 and second:
                            predict(c, cp)
                        if h == (15 if second else 14):
                            taps(cp, 1 - u)
                    dve.wait_ge(evac, n * NGI + 4 + 2 * (h + 1))
                    for g in range(2):
                        ins = v.bn_stats(ost[:, 2 * h + g, :], oc[h % 4][:, GK * g:GK * (g + 1)])
                    ins.then_inc(ostat, 1)
                assert last or c.n == links, c.n
            image_loop(dve, body)
            output_norm(Count(c0 + (NB - 1) * links + 2), Count(K_IN + (NB - 1) * K + 2), NB)


def spectrum_phase(nc, src, spectra, const):
    with ExitStack() as ctx:
        def sb(name, shape):
            return ctx.enter_context(nc.sbuf_tensor(f"{name}_sp", shape, F32))

        def sem(name):
            return ctx.enter_context(nc.semaphore(f"{name}_sp"))

        xh = [sb(f"xh{u}", [P, 2, C, W]) for u in range(2)]
        col = sb("col", [P, 4, 2 * W])
        turn = sb("turn", [P, 2, 8, P])
        xs = [sb(f"xs{u}", [2 * C, M, M]) for u in range(2)]
        fh = sb("fh", [P, 2, 2 * M])
        fw = sb("fw", [P, 2, 2, 2 * M])
        ident = sb("ident", [P, P])
        cp_ = ctx.enter_context(nc.psum_tensor("cp_sp", [P, 4, 512], F32))
        tp = ctx.enter_context(nc.psum_tensor("tp_sp", [P, 4, 4, P], F32))

        setup = sem("setup")
        loaded = [sem(f"loaded{u}") for u in range(2)]
        col_ready = sem("col_ready")
        col_act = sem("col_act")
        col_dve = sem("col_dve")
        turn_ready = sem("turn_ready")
        turn_act = sem("turn_act")
        turn_dve = sem("turn_dve")
        modes_ready = sem("modes_ready")
        modes_act = sem("modes_act")
        modes_dve = sem("modes_dve")
        stored = [sem(f"stored{u}") for u in range(2)]

        block = ctx.enter_context(nc.Block(name="spectrum"))

        def load_image(eng, n, u):
            for half in range(2):
                rows = image(src, n).rearrange("b c (f p) w -> f p (b c) w", f=2)[half]
                eng.dma_start(xh[u][:, half], rows).then_inc(loaded[u], 16)

        @block.sync
        def _(sp):
            for u in range(2):
                sp.sem_inc(stored[u], 1)
            load_image(sp, 0, 0)
            sp.dma_start(fh[:], const["fh"].rearrange("p (a b) -> p a b", a=2)).then_inc(setup, 16)
            sp.dma_start(fw[:], const["fw"].rearrange("p (a b c) -> p a b c", a=2, b=2)).then_inc(setup, 16)
            sp.dma_start(ident[:], const["ident"]).then_inc(setup, 16)
            load_image(sp, 1, 1)

            def body(n, u, last, tail):
                if not tail:
                    sp.wait_ge(col_ready, (n + 1) * 4)
                    load_image(sp, n + 2, u)
                sp.wait_ge(modes_act, n + 2)
                sp.wait_ge(modes_dve, n + 2)
                sp.dma_start(image(spectra, n).rearrange("b p (x y) -> (b p) x y", y=M), xs[u][:]).then_inc(stored[u], 16)
            image_loop(sp, body)
            for u in range(2):
                sp.wait_ge(stored[u], NB // 2 * 16 + 1)

        @block.tensor
        def _(pe):
            pe.wait_ge(setup, 48)

            def body(n, u, last, tail):
                pe.wait_ge(loaded[u], (n - u) * 16 + 32)
                pe.wait_ge(modes_act, n + 1)
                pe.wait_ge(modes_dve, n + 1)
                for nb in range(4):
                    for q in range(4):
                        for half in range(2):
                            first = 8 * nb + q
                            ins = nc.tensor.matmul(cp_[C * q:C * (q + 1), nb], fh[:, half], xh[u][:, half, first:first + 5:4, :],
                                                   start=half == 0, stop=half == 1)
                    ins.then_inc(col_ready, 1)
                for half in range(2):
                    for j in range(8):
                        if half == 0 and j == 0:
                            pe.wait_ge(col_act, 2 * n + 2)
                            pe.wait_ge(turn_act, 2 * n + 1)
                            pe.wait_ge(turn_dve, 2 * n + 1)
                        if half == 0 and j == 4:
                            pe.wait_ge(col_dve, 2 * n + 2)
                        at = (j % 2) * W + half * P
                        ins = nc.tensor.transpose(tp[:, 2 * half + j // 4, j % 4], col[:, j // 2, at:at + P], ident[:])
                        if j % 4 == 3:
                            ins.then_inc(turn_ready, 1)
                for kx in range(M):
                    for half in range(2):
                        if kx == 0:
                            pe.wait_ge(turn_act if half == 0 else turn_dve, 2 * n + 3)
                        for r in range(2):
                            lhs = turn[:, half].rearrange("p j (q r k) -> p (j q) (r k)", q=4, r=2)[:, :, r * M + kx]
                            ins = nc.tensor.matmul(cp_[0:C, 0, 2 * M * kx:2 * M * (kx + 1)], lhs, fw[:, half, r],
                                                   start=half == 0 and r == 0, stop=half == 1 and r == 1)
                ins.then_inc(modes_ready, 1)
            image_loop(pe, body)

        def evacuate(eng, copy, mine, col_done, turn_done, modes_done):
            eng.sem_inc(turn_done, 1)
            eng.sem_inc(modes_done, 1)

            def body(n, u, last, tail):
                for k in range(2):
                    nb = 2 * mine + k
                    eng.wait_ge(col_ready, 4 * n + nb + 1)
                    copy(col[:, nb], cp_[:, nb]).then_inc(col_done, 1)
                for k in range(2):
                    eng.wait_ge(turn_ready, 4 * n + 2 * mine + k + 1)
                    copy(turn[:, mine, 4 * k:4 * k + 4], tp[:, 2 * mine + k]).then_inc(turn_done, 1)
                if mine:
                    eng.wait_ge(modes_act, n + 2)
                eng.wait_ge(modes_ready, n + 1)
                eng.wait_ge(stored[u], (n - u) * 8 + 1)
                modes = cp_[0:C, 0].rearrange("p (x r y) -> p r x y", r=2, y=M)
                copy(xs[u][C * mine:C * (mine + 1)], modes[:, mine]).then_inc(modes_done, 1)
            image_loop(eng, body)

        @block.scalar
        def _(act):
            evacuate(act, lambda o, i: nc.scalar.activation(o, i, ACT.Copy), 0, col_act, turn_act, modes_act)

        @block.vector
        def _(dve):
            evacuate(dve, lambda o, i: nc.vector.tensor_copy(o, i), 1, col_dve, turn_dve, modes_dve)


def mixing_phase(nc, spectra, stats, weights, mixed):
    with ExitStack() as ctx:
        def sb(name, shape):
            return ctx.enter_context(nc.sbuf_tensor(f"{name}_mx", shape, F32))

        def sem(name):
            return ctx.enter_context(nc.semaphore(f"{name}_mx"))

        wm = sb("wm", [2 * C, C, MM, 2])
        wr = sb("wr", [2 * C, C, MM, 2])
        x = sb("x", [2 * C, NB, MM])
        o = sb("o", [2 * C, NB, MM])
        st = sb("st", [2 * C, NB, 2])
        veps, root, inv, half, scl = (sb(n, [2 * C, NB]) for n in ("veps", "root", "inv", "half", "scl"))
        ps = ctx.enter_context(nc.psum_tensor("ps_mx", [2 * C, 8, 32, 16], F32))
        loaded = sem("loaded")
        w_loaded = sem("w_loaded")
        link = sem("link")
        root_ready = sem("root_ready")
        x_ready = sem("x_ready")
        w_act = sem("w_act")
        w_dve = sem("w_dve")
        ready = sem("ready")
        o_act = sem("o_act")
        o_dve = sem("o_dve")
        stored = sem("stored")
        block = ctx.enter_context(nc.Block(name="mixing"))

        @block.sync
        def _(sp):
            sp.dma_start(x[:], spectra.rearrange("b p m -> p b m")).then_inc(loaded, 16)
            for r in range(2):
                sp.dma_start(st[C * r:C * (r + 1)], stats.rearrange("b c s -> c b s")).then_inc(loaded, 16)
            w = weights.rearrange("i o x y r -> i o (x y) r")
            for part in range(4):
                of = slice(8 * part, 8 * part + 8)
                sp.dma_start(wr[C:2 * C, of], w[:, of]).then_inc(w_loaded, 16)
                sp.dma_start(wm[0:C, of], w[:, of]).then_inc(w_loaded, 16)
            sp.wait_ge(o_act, 4)
            sp.wait_ge(o_dve, 4)
            sp.dma_start(mixed.rearrange("b p m -> p b m"), o[:]).then_inc(stored, 16)
            sp.wait_ge(stored, 16)

        @block.vector
        def _(dve):
            v = nc.vector
            dve.wait_ge(loaded, 48)
            v.tensor_scalar(veps[:], st[:, :, 1], EPS, None, ALU.add).then_inc(link, 1)
            v.scalar_tensor_tensor(out=x[0:C, :, 0], in0=st[0:C, :, 0], scalar=-float(H * W), in1=x[0:C, :, 0],
                                   op0=ALU.mult, op1=ALU.add)
            dve.wait_ge(root_ready, 1)
            v.reciprocal(inv[:], root[:]).then_inc(link, 1)
            dve.wait_ge(link, 2)
            v.tensor_tensor(half[:], inv[:], inv[:], ALU.mult).then_inc(link, 1)
            dve.wait_ge(link, 3)
            v.tensor_tensor(half[:], half[:], veps[:], ALU.mult).then_inc(link, 1)
            dve.wait_ge(link, 4)
            v.tensor_scalar(half[:], half[:], -0.5, 1.5, ALU.mult, ALU.add).then_inc(link, 1)
            dve.wait_ge(link, 5)
            v.tensor_tensor(scl[:], inv[:], half[:], ALU.mult).then_inc(link, 1)
            dve.wait_ge(link, 6)
            v.tensor_tensor(x[:], x[:], scl[:].unsqueeze(2).broadcast_to([2 * C, NB, MM]), ALU.mult).then_inc(x_ready, 1)
            dve.wait_ge(w_loaded, 128)
            v.tensor_copy(wm[C:2 * C, :, :, 1], wr[C:2 * C, :, :, 0]).then_inc(w_dve, 1)
            for k in range(1, 8, 2):
                dve.wait_ge(ready, k + 1)
                v.tensor_copy(o[:, :, 32 * k:32 * k + 32], ps[:, k, :, 0:NB].rearrange("p m b -> p b m")).then_inc(o_dve, 1)

        @block.scalar
        def _(act):
            act.wait_ge(link, 1)
            nc.scalar.activation(root[:], veps[:], ACT.Sqrt).then_inc(root_ready, 1)
            act.wait_ge(w_loaded, 128)
            nc.scalar.activation(wm[C:2 * C, :, :, 0], wr[C:2 * C, :, :, 1], ACT.Copy, scale=-1.0).then_inc(w_act, 1)
            for k in range(0, 8, 2):
                act.wait_ge(ready, k + 1)
                nc.scalar.activation(o[:, :, 32 * k:32 * k + 32], ps[:, k, :, 0:NB].rearrange("p m b -> p b m"), ACT.Copy).then_inc(o_act, 1)

        @block.tensor
        def _(pe):
            pe.wait_ge(w_act, 1)
            pe.wait_ge(w_dve, 1)
            pe.wait_ge(x_ready, 1)
            for m in range(MM):
                for r in range(2):
                    ins = nc.tensor.matmul(ps[C * r:C * (r + 1), m // 32, m % 32, 0:NB], wm[:, :, m, r], x[:, :, m],
                                           start=True, stop=True)
                if m % 32 == 31:
                    ins.then_inc(ready, 1)


GH = 2
GB = S
STEPS = W
BLOCKS = STEPS // T
OUT, FORGET, IN, CELL = range(4)


def lstm_phase(nc, src, out, stats, par, const):
    with ExitStack() as ctx:
        def sb(name, shape):
            return ctx.enter_context(nc.sbuf_tensor(f"{name}_ls", shape, F32))

        def sem(name):
            return ctx.enter_context(nc.semaphore(f"{name}_ls"))

        def sems(name):
            return [sem(f"{name}{k}") for k in range(2)]

        xs = [sb(f"xs{k}", [P, GH, H, T + 1]) for k in range(2)]
        ys = [sb(f"ys{k}", [P, GH, H, T]) for k in range(2)]
        stack = sb("stack", [P, 2, GH, 2, H + 1])
        hid = sb("hid", [P, 2, GH, H])
        cell = sb("cell", [P, GH, H])
        gate = sb("gate", [P, GH, 4, H])
        fc, ig, tc = (sb(n, [P, GH, H]) for n in ("fc", "ig", "tc"))
        below = sb("below", [P, GH, T])
        w2d = sb("w2d", [P, 4, P])
        w2n = sb("w2n", [P, GH, 4, P])
        w1d = sb("w1d", [P, 2, 4, P])
        own = sb("own", [P, GH, 2, 4, 2 * C])
        above = sb("above", [P, 2, 4, 2 * C])
        w2raw = sb("w2raw", [P, C])
        w1raw = sb("w1raw", [P, C, 2])
        b1row, b2row, brow = (sb(n, [4, C]) for n in ("b1row", "b2row", "brow"))
        b12 = sb("b12", [P, 4])
        bias = sb("bias", [P, GH, 4])
        st = sb("st", [P, GH, 2])
        veps, root, inv, half, scl = (sb(n, [P, GH]) for n in ("veps", "root", "inv", "half", "scl"))
        ident = sb("ident", [P, P])
        ps = ctx.enter_context(nc.psum_tensor("ps_ls", [P, GH, 4, 512], F32))
        small = ps[:, 0, 0]

        setup = sem("setup")
        passed = sem("passed")
        turned = sem("turned")
        ready = sem("ready")
        zeroed = sem("zeroed")
        link = sem("link")
        st_loaded = sem("st_loaded")
        root_ready = sem("root_ready")
        veps_ready = sem("veps_ready")
        scl_ready = sem("scl_ready")
        w2n_ready = sem("w2n_ready")
        mean_ready = sem("mean_ready")
        bias_ready = sem("bias_ready")
        xs_loaded, ys_loaded, ys_stored = sems("xs_loaded"), sems("ys_loaded"), sems("ys_stored")
        sums_ready = sems("sums_ready")
        gates_ready = sems("gates_ready")
        parts_ready = sems("parts_ready")
        cell_ready = sems("cell_ready")
        tanh_ready = sems("tanh_ready")
        stack_ready = sems("stack_ready")
        hid_ready = sems("hid_ready")
        added = sems("added")
        block_done = sems("block_done")

        rows_of = [min(H, T * (tb + 1) + 1) for tb in range(BLOCKS)]
        order = (FORGET, IN, CELL, OUT)
        pairs = [slice(2 * C * j, 2 * C * (j + 1)) for j in range(2)]
        hidden_at = [pairs[1], pairs[0]]

        def steps(eng, hf, tb, body):
            eng.sem_inc(passed, 1)
            with eng.Fori(0, T // 2) as i:
                for parity in range(2):
                    body(hf * STEPS + (tb * T + 2 * i + parity), 2 * i + parity, parity)

        def stacks(hf, tb, steps_done):
            return hf * (STEPS + BLOCKS) + (2 + tb + steps_done)

        def groups_of(t, hf, g):
            return t[bass.ds(hf * (GH * GB) + GB * g, GB)]

        block = ctx.enter_context(nc.Block(name="lstm"))

        @block.sync
        def _(sp):
            for p in range(2):
                sp.sem_inc(ys_stored[p], 1)
            sp.dma_start(ident[:], const["ident"]).then_inc(setup, 16)
            sp.dma_start(w2raw[:], par["W2"]).then_inc(setup, 16)
            sp.dma_start(w1raw[:], par["W1"]).then_inc(setup, 16)
            sp.dma_start(b1row[:], par["b1"].rearrange("(k o) -> k o", k=4)).then_inc(setup, 16)
            sp.dma_start(b2row[:], par["b2"].rearrange("(k o) -> k o", k=4)).then_inc(setup, 16)

            with sp.Fori(0, 2) as hf:
                def load(tb):
                    p, n, t0 = tb % 2, rows_of[tb], T * tb
                    for g in range(GH):
                        if tb >= 2:
                            sp.wait_ge(stack_ready[g], stacks(hf, tb - 2, T * (tb - 1)))
                        else:
                            sp.wait_ge(stack_ready[g], hf * (STEPS + BLOCKS) + 1)
                    sp.sem_inc(passed, 1)
                    for g in range(GH):
                        skewed = groups_of(src, hf, g).rearrange("b c h w -> (b c) (h w)")[:, PAD + t0:PAD + t0 + n * (WX - 1)]
                        sp.dma_start(xs[p][:, g, 0:n, :], skewed.rearrange("p (h w) -> p h w", w=WX - 1)[:, :, 0:T + 1]).then_inc(xs_loaded[p], 16)
                    sp.wait_ge(ys_stored[p], (hf * (BLOCKS // 2) + tb // 2) * 32 + 1)
                    for g in range(GH):
                        cells = groups_of(src, hf, g).rearrange("b c h w -> (b c) h w")[:, :, PAD + t0:PAD + t0 + T]
                        sp.dma_start(ys[p][:, g], cells).then_inc(ys_loaded[p], 16)

                sp.wait_ge(bias_ready, hf + 1)
                sp.sem_inc(passed, 1)
                for g in range(GH):
                    sp.dma_start(st[:, g], groups_of(stats, hf, g).rearrange("b c s -> (b c) s")).then_inc(st_loaded, 16)
                load(0)
                for tb in range(BLOCKS):
                    if tb + 1 < BLOCKS:
                        load(tb + 1)
                    for g in range(GH):
                        sp.wait_ge(block_done[g], hf * BLOCKS + tb + 2)
                        cells = groups_of(out, hf, g).rearrange("b c h w -> (b c) h w")[:, :, T * tb:T * (tb + 1)]
                        sp.dma_start(cells, ys[tb % 2][:, g]).then_inc(ys_stored[tb % 2], 16)
            for p in range(2):
                sp.wait_ge(ys_stored[p], BLOCKS * 32 + 1)

        @block.tensor
        def _(pe):
            pe.wait_ge(setup, 80)
            pe.wait_ge(link, 1)
            nc.tensor.transpose(small[0:C, 0:P], w2raw[:], ident[:])
            for j in range(2):
                nc.tensor.transpose(small[0:C, P * (1 + j):P * (2 + j)], w1raw[:, :, j], ident[:])
            nc.tensor.transpose(ps[0:C, 1, 0, 0:4], brow[:], ident[0:4, 0:4]).then_inc(turned, 1)
            pe.wait_ge(ready, 1)

            with pe.Fori(0, 2) as hf:
                pe.wait_ge(w2n_ready, hf + 1)
                for g in range(GH):
                    for k in range(4):
                        ins = nc.tensor.matmul(small[:, 4 * g + k:4 * g + k + 1], w2n[:, g, k], st[:, g, 0:1], start=True, stop=True)
                ins.then_inc(mean_ready, 1)
                pe.wait_ge(bias_ready, hf + 2)
                for tb in range(BLOCKS):
                    n = rows_of[tb]

                    def step(done, tau, parity):
                        for g in range(GH):
                            pe.wait_ge(stack_ready[g], hf * BLOCKS + 2 + tb + done)
                            for k in order:
                                for j in range(2):
                                    to, x = ps[pairs[j], g, k, 0:n], stack[:, parity, g, j]
                                    nc.tensor.matmul(to, own[:, g, j, k], x[:, 1:n + 1], start=True, stop=False)
                                    ins = nc.tensor.matmul(to, above[:, j, k], x[:, 0:n], start=False, stop=True)
                                ins.then_inc(sums_ready[g], 1)
                    steps(pe, hf, tb, step)

        @block.scalar
        def _(act):
            with act.Fori(0, 2) as hf:
                act.wait_ge(veps_ready, hf + 1)
                nc.scalar.activation(root[:], veps[:], ACT.Sqrt).then_inc(root_ready, 1)
                act.wait_ge(bias_ready, hf + 2)
                for tb in range(BLOCKS):
                    n = rows_of[tb]

                    def step(done, tau, parity):
                        for g in range(GH):
                            for at, k in enumerate(order):
                                act.wait_ge(sums_ready[g], done * 4 + (at + 1))
                                if k == OUT:
                                    act.wait_ge(hid_ready[g], done + 1)
                                f = ACT.Tanh if k == CELL else ACT.Sigmoid
                                nc.scalar.activation(gate[:, g, k, 0:n], ps[:, g, k, 0:n], f,
                                                     bias=bias[:, g, k:k + 1]).then_inc(gates_ready[g], 1)
                            act.wait_ge(cell_ready[g], done + 1)
                            nc.scalar.activation(tc[:, g, 0:n], cell[:, g, 0:n], ACT.Tanh).then_inc(tanh_ready[g], 1)
                    steps(act, hf, tb, step)

        @block.vector
        def _(dve):
            v = nc.vector
            dve.sem_inc(bias_ready, 1)
            for g in range(GH):
                dve.sem_inc(stack_ready[g], 1)
                dve.sem_inc(hid_ready[g], 1)
            v.memset(w2d[:], 0.0)
            v.memset(w1d[:], 0.0)
            v.memset(above[:], 0.0)
            dve.wait_ge(setup, 80)
            v.tensor_tensor(brow[:], b1row[:], b2row[:], ALU.add).then_inc(link, 1)
            dve.wait_ge(link, 1)
            dve.wait_ge(turned, 1)
            for q in range(GB):
                here = slice(C * q, C * (q + 1))
                v.tensor_copy(w2d[here, :, here], small[0:C, 0:P].rearrange("p (k o) -> p k o", k=4))
                for j in range(2):
                    v.tensor_copy(w1d[here, j, :, here], small[0:C, P * (1 + j):P * (2 + j)].rearrange("p (k o) -> p k o", k=4))
                ins = v.tensor_copy(b12[here, :], ps[0:C, 1, 0, 0:4])
            ins.then_inc(ready, 1)
            dve.wait_ge(ready, 1)
            for j in range(2):
                v.tensor_copy(above[hidden_at[j], j], w1d[pairs[j], 0, :, pairs[j]])
                for g in range(GH):
                    ins = v.tensor_copy(own[hidden_at[j], g, j], w1d[pairs[j], 1, :, pairs[j]])
            ins.then_inc(ready, 1)
            dve.wait_ge(ready, 2)

            with dve.Fori(0, 2) as hf:
                c = Count(hf * 5 + 1)

                def chained(ins):
                    ins.then_inc(link, 1)
                    dve.wait_ge(link, c.next())

                dve.wait_ge(st_loaded, hf * 32 + 32)
                chained(v.tensor_scalar(veps[:], st[:, :, 1], EPS, None, ALU.add))
                dve.sem_inc(veps_ready, 1)
                dve.wait_ge(root_ready, hf + 1)
                chained(v.reciprocal(inv[:], root[:]))
                chained(v.tensor_tensor(half[:], inv[:], inv[:], ALU.mult))
                chained(v.tensor_tensor(half[:], half[:], veps[:], ALU.mult))
                chained(v.tensor_scalar(half[:], half[:], -0.5, 1.5, ALU.mult, ALU.add))
                v.tensor_tensor(scl[:], inv[:], half[:], ALU.mult).then_inc(scl_ready, 1)
                dve.wait_ge(scl_ready, hf + 1)
                for g in range(GH):
                    ins = v.tensor_scalar(w2n[:, g], w2d[:], scl[:, g:g + 1], None, ALU.mult)
                ins.then_inc(w2n_ready, 1)
                dve.wait_ge(w2n_ready, hf + 1)
                for g in range(GH):
                    for j in range(2):
                        v.tensor_copy(own[pairs[j], g, j], w2n[pairs[j], g, :, pairs[j]])
                dve.wait_ge(mean_ready, hf + 1)
                for g in range(GH):
                    ins = v.tensor_tensor(bias[:, g], b12[:], small[:, 4 * g:4 * g + 4], ALU.subtract)
                ins.then_inc(bias_ready, 1)
                v.memset(cell[:], 0.0)
                v.memset(stack[:], 0.0).then_inc(zeroed, 1)
                dve.wait_ge(zeroed, hf + 1)
                for tb in range(BLOCKS):
                    n, p = rows_of[tb], tb % 2
                    m = rows_of[tb - 1] if tb else 0
                    dve.wait_ge(xs_loaded[p], (hf * (BLOCKS // 2) + tb // 2 + 1) * 32)
                    for g in range(GH):
                        if tb:
                            dve.wait_ge(stack_ready[g], stacks(hf, tb - 1, T * tb))
                            v.tensor_copy(cell[:, g, m:n], cell[:, g, m - 1:m].broadcast_to([P, n - m]))
                            for j in range(2):
                                h = stack[hidden_at[j], 0, g, j]
                                v.tensor_copy(h[:, m + 1:n + 1], h[:, m:m + 1].broadcast_to([2 * C, n - m]))
                        for j in range(2):
                            ins = v.tensor_copy(stack[pairs[j], 0, g, j, m + 1:n + 1], xs[p][pairs[j], g, m:n, 0])
                        ins.then_inc(stack_ready[g], 1)
                    for g in range(GH):
                        dve.wait_ge(stack_ready[g], stacks(hf, tb, T * tb))

                    def step(done, tau, parity):
                        for g in range(GH):
                            dve.wait_ge(gates_ready[g], done * 4 + 1)
                            v.tensor_tensor(fc[:, g, 0:n], gate[:, g, FORGET, 0:n], cell[:, g, 0:n], ALU.mult)
                            dve.wait_ge(gates_ready[g], done * 4 + 3)
                            v.tensor_tensor(ig[:, g, 0:n], gate[:, g, IN, 0:n], gate[:, g, CELL, 0:n], ALU.mult).then_inc(parts_ready[g], 1)
                            dve.wait_ge(parts_ready[g], done + 1)
                            v.tensor_tensor(cell[:, g, 0:n], fc[:, g, 0:n], ig[:, g, 0:n], ALU.add).then_inc(cell_ready[g], 1)
                            for j in range(2):
                                v.tensor_copy(stack[pairs[j], 1 - parity, g, j, 1:n + 1],
                                              xs[p][pairs[j], g, 0:n, bass.ds(tau + 1, 1)].rearrange("p h t -> p (h t)"))
                            dve.wait_ge(gates_ready[g], done * 4 + 4)
                            dve.wait_ge(tanh_ready[g], done + 1)
                            for j in range(2):
                                ins = v.tensor_tensor(stack[hidden_at[j], 1 - parity, g, j, 1:n + 1],
                                                      gate[pairs[j], g, OUT, 0:n], tc[pairs[j], g, 0:n], ALU.mult)
                            ins.then_inc(stack_ready[g], 1)
                            dve.wait_ge(added[g], done + 1)
                            v.tensor_tensor(hid[:, parity, g, 0:n], gate[:, g, OUT, 0:n], tc[:, g, 0:n], ALU.mult).then_inc(hid_ready[g], 1)
                    steps(dve, hf, tb, step)

        @block.gpsimd
        def _(pl):
            v = nc.gpsimd
            for g in range(GH):
                pl.sem_inc(added[g], 2)
                pl.sem_inc(block_done[g], 1)
            with pl.Fori(0, 2) as hf:
                for tb in range(BLOCKS):
                    n, p = rows_of[tb], tb % 2
                    pl.wait_ge(ys_loaded[p], (hf * (BLOCKS // 2) + tb // 2 + 1) * 32)
                    for g in range(GH):
                        pl.wait_ge(block_done[g], hf * BLOCKS + tb + 1)

                    def step(done, tau, parity):
                        for g in range(GH):
                            pl.wait_ge(hid_ready[g], done + 2)
                            if n < H:
                                v.tensor_copy(below[:, g, bass.ds(tau, 1)], hid[:, parity, g, n - 1:n])
                            cells = ys[p][:, g, 0:n, bass.ds(tau, 1)].rearrange("p h t -> p (h t)")
                            v.tensor_tensor(cells, cells, hid[:, parity, g, 0:n], ALU.add).then_inc(added[g], 1)
                    steps(pl, hf, tb, step)
                    for g in range(GH):
                        pl.wait_ge(added[g], hf * STEPS + T * (tb + 1) + 2)
                        if n < H:
                            cells = ys[p][:, g, n:H, :]
                            v.tensor_tensor(cells, cells, below[:, g].unsqueeze(1).broadcast_to([P, H - n, T]), ALU.add).then_inc(block_done[g], 1)
                        else:
                            pl.sem_inc(block_done[g], 1)


def program(nc, x, const, out):
    x1 = nc.dram_tensor("x1", (NB, C, H, W), F32).ap()
    x3 = nc.dram_tensor("x3", (NB, C, H, WX), F32).ap()
    stats1 = nc.dram_tensor("stats1", (NB, C, 2), F32).ap()
    stats3 = nc.dram_tensor("stats3", (NB, C, 2), F32).ap()
    spectra = nc.dram_tensor("spectra", (NB, 2 * C, MM), F32).ap()
    mixed = nc.dram_tensor("mixed", (NB, 2 * C, MM), F32).ap()
    conv_phase(nc, 0, x["x"], x1, stats1, None, const, {"w": x["L0_conv_weight"]})
    spectrum_phase(nc, x1, spectra, const)
    mixing_phase(nc, spectra, stats1, x["L1_conv_weights1"], mixed)
    conv_phase(nc, 2, x1, x3, stats3, mixed, const,
               {"w1": x["L2_conv_w1"], "b1": x["L2_conv_b1"], "w2": x["L2_conv_w2"], "b2": x["L2_conv_b2"]})
    lstm_phase(nc, x3, out, stats3,
               {"W2": x["L3_conv_W2"], "W1": x["L3_conv_W1"], "b1": x["L3_conv_b1"], "b2": x["L3_conv_b2"]}, const)


def constants():
    import numpy as np
    p = np.arange(P)
    f = np.float64
    k = np.arange(M)
    ang_h = 2 * np.pi * np.outer(np.arange(H), k) / H
    ang_w = 2 * np.pi * np.outer(np.arange(W), k) / W
    i3 = np.zeros((P, 3, 2, C))
    for i in range(2):
        i3[C * (i + 1):C * (i + 2), 1, i, :] = np.eye(C)
    fh = np.concatenate([np.cos(ang_h), -np.sin(ang_h)], 1).reshape(2, P, 2 * M).transpose(1, 0, 2)
    fw = np.stack([np.concatenate([np.cos(ang_w), -np.sin(ang_w)], 1),
                   np.concatenate([np.sin(ang_w), np.cos(ang_w)], 1)], 1).reshape(2, P, 2, 2 * M).transpose(1, 0, 2, 3)
    eh = np.zeros((2 * C, H))
    eh[0:M] = np.cos(ang_h).T
    eh[C:C + M] = np.sin(ang_h).T
    twice = np.where(k == 0, 1.0, 2.0)[:, None] / (H * W)
    ew = np.concatenate([twice * np.cos(ang_w).T, -twice * np.sin(ang_w).T], 0)
    t = {
        "ident": np.eye(P),
        "g8": ((p[:, None] % C) // 2 == (p[None, :] % C) // 2) / 8.0,
        "g4": (p[:, None] % C == p[None, :] % C) / 4.0,
        "i3": i3.reshape(P, -1),
        "i4": (p[:, None] % C == np.arange(C)[None, :]) * 1.0,
        "ones": np.ones((P, PAD)),
        "fh": fh.reshape(P, -1), "fw": fw.reshape(P, -1), "eh": eh, "ew": ew,
    }
    return {n: np.ascontiguousarray(a, dtype=np.float32) for n, a in t.items()}


_INS = ['x', 'L0_conv_weight', 'L1_conv_weights1', 'L1_conv_weights2', 'L2_conv_w1', 'L2_conv_b1', 'L2_conv_w2',
        'L2_conv_b2', 'L3_conv_W2', 'L3_conv_b2', 'L3_conv_W1', 'L3_conv_b1']


def kernel(**inputs):
    import numpy as _np
    import concourse.bacc as _bacc
    from concourse import mybir as _mybir
    from concourse.bass_utils import run_bass_kernel_spmd as _run

    nc = _bacc.Bacc("TRN2", target_bir_lowering=False, num_devices=1)
    arrays, args, const = {}, {}, {}
    for name in _INS:
        a = _np.ascontiguousarray(inputs[name])
        arrays[f"in_{name}_dram"] = a
        args[name] = nc.dram_tensor(f"in_{name}_dram", a.shape, _mybir.dt.from_np(a.dtype), kind="ExternalInput").ap()
    for name, a in constants().items():
        arrays[f"const_{name}_dram"] = a
        const[name] = nc.dram_tensor(f"const_{name}_dram", a.shape, _mybir.dt.from_np(a.dtype), kind="ExternalInput").ap()
    out = nc.dram_tensor("out_0_dram", (NB, C, H, W), F32, kind="ExternalOutput").ap()
    program(nc, args, const, out)
    r = _run(nc, [arrays], core_ids=[0])
    return r.results[0]["out_0_dram"]
```

```python
from contextlib import ExitStack

import concourse.bass as bass
from concourse import mybir

F32 = mybir.dt.float32
ALU = mybir.AluOpType
ACT = mybir.ActivationFunctionType

NB, C, H, W = 16, 32, 256, 256
P = 128
S = P // C
KB = H // S
WP = W + 2
CK = 8
NCH = KB // CK
GK = 2
NG = CK // GK
NGI = NCH * NG
M = 16
MM = M * M
T = 16
PAD = 16
WX = PAD + W
EPS = 1e-5


DIV = float((C * 9) ** 0.5)
HC = 2 * NCH
HB = CK // 2


class Count:

    def __init__(self, base):
        self.base, self.n = base, 0

    def next(self):
        self.n += 1
        return self.base + self.n


def image_loop(eng, body):
    with eng.Fori(0, NB // 2 - 1) as i:
        for u in range(2):
            body(i * 2 + u, u, False, False)
    body(NB - 2, 0, False, True)
    body(NB - 1, 1, True, True)


def image(t, n):
    return t[bass.ds(n, 1)]


def conv_phase(nc, layer, src, dst, stats, spectra, const, par):
    second = layer == 2
    left = PAD if second else 0
    with ExitStack() as ctx:
        def sb(name, shape):
            return ctx.enter_context(nc.sbuf_tensor(f"{name}_l{layer}", shape, F32))

        def sem(name):
            return ctx.enter_context(nc.semaphore(f"{name}_l{layer}"))

        xa = [sb(f"xa{u}", [P, KB + 1, WP]) for u in range(2)]
        xb = [sb(f"xb{u}", [P, HB, WP]) for u in range(4)]
        xt = [sb(f"xt{u}", [P, WP]) for u in range(2)]
        oc = [sb(f"oc{u}", [P, HB, W]) for u in range(4)]
        ist = sb("ist", [P, NGI, 6])
        ost = sb("ost", [P, NGI, 6])
        agg_i = sb("agg_i", [P, 2])
        agg_o = sb("agg_o", [P, 2])
        grp_i = sb("grp_i", [P, 2])
        grp_o = sb("grp_o", [P, 2])
        scl = sb("scl", [P, 1])
        veps, root, inv, half = (sb(x, [P, 1]) for x in ("veps", "root", "inv", "half"))
        dev = sb("dev", [P, 1])
        var = sb("var", [P, 1])
        wn = sb("wn", [P, 3, 2, C])
        wf = [sb(f"wf{u}", [P, 3, 2, C]) for u in range(2)]
        nb = [sb(f"nb{u}", [P, 1]) for u in range(2)]
        ones = sb("ones", [P, WP])
        g8 = sb("g8", [P, P])
        i3 = sb("i3", [P, 3, 2, C])
        if not second:
            wraw = sb("wraw", [C, C, 3, 3])
            ident = sb("ident", [C, C])
            wb = sb("wb", [P, 3, 2, C])
        else:
            ident = sb("ident", [2 * C, 2 * C])
            g4 = sb("g4", [P, P])
            i4 = sb("i4", [P, C])
            w1 = sb("w1", [C, P])
            b1 = sb("b1", [P, 1])
            w2raw = sb("w2raw", [P, C, 3, 3])
            w2r = sb("w2r", [P, 3, 2, S, C])
            b2c = sb("b2c", [C, 3, 3])
            b2r = sb("b2r", [P, 3, 2])
            pool = sb("pool", [P, 1])
            hdn = sb("hdn", [P, 1])
            kern = sb("kern", [P, 6])
            kn = sb("kn", [P, 6])
            mpad = sb("mpad", [P, PAD])
            mpads = sb("mpads", [P, KB, PAD])
            o1 = [sb(f"o1{u}", [2 * C, M, M]) for u in range(2)]
            tt = sb("tt", [2 * C, C, 2, M])
            eh = sb("eh", [2 * C, H])
            ew = sb("ew", [C, W])
            gs = sb("gs", [C, H // 2, C])

        cps = ctx.enter_context(nc.psum_tensor(f"cps_l{layer}", [P, 4, GK, W], F32))
        yps = ctx.enter_context(nc.psum_tensor(f"yps_l{layer}", [P, 3, GK, W], F32))
        sm = ctx.enter_context(nc.psum_tensor(f"sm_l{layer}", [P, 512], F32))

        passed = sem("passed")
        setup = sem("setup")
        turned = sem("turned")
        ready = sem("ready")
        xa_loaded = [[sem(f"xa_loaded{u}_{j}") for j in range(NCH // 2)] for u in range(2)]
        xa_final = sem("xa_final")
        taps_ready = sem("taps_ready")
        xb_loaded = [sem(f"xb_loaded{u}") for u in range(4)]
        xt_loaded = [sem(f"xt_loaded{u}") for u in range(2)]
        conv_ready = sem("conv_ready")
        evac = sem("evac")
        ostat = sem("ostat")
        istat = sem("istat")
        stored = [sem(f"stored{u}") for u in range(4)]
        link = sem("link")
        v2p = sem("v2p")
        p2v = sem("p2v")
        var_ready = sem("var_ready")
        root_ready = sem("root_ready")
        nb_ready = sem("nb_ready")
        grp_ready = sem("grp_ready")
        grp_stored = sem("grp_stored")
        o1_loaded = [sem(f"o1_loaded{u}") for u in range(2)]
        t_ready = sem("t_ready")
        t_copied = sem("t_copied")
        g_ready = sem("g_ready")
        g_copied = sem("g_copied")
        y_ready = sem("y_ready")
        y_added = sem("y_added")

        K_IN = 5 if second else 3
        K = K_IN + 2
        N_SETUP = 16 * (12 if second else 4)
        banks_of = [0] * 3 + [4] * 4 + [0] * 2 + [4] * 4 + [0] * 3 if second else [4] * 8 + [0] * 8
        spectra_at = {(1, 0): (0, 0), (1, 1): (0, 2), (2, 0): (0, 4), (2, 1): (0, 6),
                      (7, 1): (1, 0), (8, 0): (1, 2), (8, 1): (1, 4), (9, 0): (1, 6)} if second else {}
        starts = [sum(banks_of[:h]) for h in range(HC)]

        def load_chunk(eng, n, u, j):
            for s in range(S):
                rows = image(src, n).rearrange("b c (k s) w -> s (b c) k w", s=S)[s][:, CK * j:CK * (j + 1)]
                eng.dma_start(xa[u][C * s:C * (s + 1), CK * j:CK * (j + 1), 1:W + 1], rows).then_inc(xa_loaded[u][j // 2], 16)

        block = ctx.enter_context(nc.Block(name=f"conv{layer}"))

        @block.sync
        def _(sp):
            for o in range(4):
                sp.sem_inc(stored[o], 1)
            sp.sem_inc(grp_stored, 16 * (1 + S * second) + 1)
            for u in range(2):
                for j in range(NCH):
                    load_chunk(sp, u, u, j)

            def body(n, u, last, tail):
                for h in range(HC):
                    sp.wait_ge(evac, n * NGI + 4 + 2 * (h + 1))
                    o = h % 4
                    for s in range(S):
                        blocks = HB - (h == HC - 1 and s == S - 1)
                        r0 = h * HB * S + 1 + s
                        rows = image(dst, n)[:, :, r0:r0 + (blocks - 1) * S + 1:S, left:left + W]
                        sp.dma_start(rows.rearrange("b c k w -> (b c) k w"),
                                     oc[o][C * s:C * (s + 1), 0:blocks, :]).then_inc(stored[o], 16)
                    if h == HC - 1:
                        row = image(dst, n)[:, :, 0:1, left:left + W]
                        sp.dma_start(row.rearrange("b c k w -> (b c) k w"),
                                     oc[o][3 * C:P, HB - 1:HB, :]).then_inc(stored[o], 16)
                    if h % 2 == 1 and not tail:
                        load_chunk(sp, n + 2, u, h // 2)
                sp.wait_ge(grp_ready, n + 2)
                sp.dma_start(image(stats, n).rearrange("b c s -> (b c) s"), grp_o[0:C, :]).then_inc(grp_stored, 16)
                if second:
                    for s in range(S):
                        cells = image(dst, n).rearrange("b c (k s) w -> s (b c) k w", s=S)[s][:, :, 0:PAD]
                        sp.dma_start(cells, mpads[C * s:C * (s + 1)]).then_inc(grp_stored, 16)

            image_loop(sp, body)
            for o in range(4):
                sp.wait_ge(stored[o], NB * 16 * (4 * S + (o == 3)) + 1)
            sp.wait_ge(grp_stored, (NB + 1) * 16 * (1 + S * second) + 1)

        @block.gpsimd
        def _(pl):
            if second:
                for u in range(2):
                    pl.dma_start(o1[u][:], spectra[u].rearrange("p (x y) -> p x y", y=M)).then_inc(o1_loaded[u], 16)

            def body(n, u, last, tail):
                if second and not tail:
                    pl.wait_ge(t_ready, n + 1)
                    pl.sem_inc(passed, 1)
                    pl.dma_start(o1[u][:], image(spectra, n + 2).rearrange("b p (x y) -> (b p) x y", y=M)).then_inc(o1_loaded[u], 16)
                pl.wait_ge(xa_final, n + 1)
                pl.sem_inc(passed, 1)
                pl.dma_start(xt[u][2 * C:P, :], xa[u][0:2 * C, 0, :]).then_inc(xt_loaded[u], 16)
                for h in range(HC):
                    pl.wait_ge(conv_ready, n * NGI + 2 * h + 2)
                    pl.sem_inc(passed, 1)
                    k = HB * h
                    pl.dma_start(xb[h % 4][0:2 * C], xa[u][2 * C:P, k:k + HB, :]).then_inc(xb_loaded[h % 4], 16)
                    pl.dma_start(xb[h % 4][2 * C:P], xa[u][0:2 * C, k + 1:k + HB + 1, :]).then_inc(xb_loaded[h % 4], 16)
            image_loop(pl, body)

        @block.tensor
        def _(pe):
            def input_mean(c):
                pe.wait_ge(v2p, c.next())
                if second:
                    nc.tensor.matmul(sm[:, 2:3], g4[:], agg_i[:, 0:1], start=True, stop=True)
                nc.tensor.matmul(sm[:, 0:1], g8[:], agg_i[:, 0:1], start=True, stop=True).then_inc(p2v, 1)

            def output_mean(c):
                pe.wait_ge(v2p, c.next())
                nc.tensor.matmul(sm[:, 0:1], g8[:], agg_o[:, 0:1], start=True, stop=True).then_inc(p2v, 1)

            def variance(c):
                pe.wait_ge(v2p, c.next())
                nc.tensor.matmul(sm[:, 1:2], g8[:], var[:], start=True, stop=True).then_inc(p2v, 1)

            def hidden(c):
                pe.wait_ge(v2p, c.next())
                nc.tensor.matmul(sm[:, 3:4], w1[:], pool[0:C, :], start=True, stop=True).then_inc(p2v, 1)

            def predicted(c):
                pe.wait_ge(v2p, c.next())
                for t in range(6):
                    ins = nc.tensor.matmul(sm[:, 4 + t:5 + t], w2r[:, t // 2, t % 2], hdn[:], start=True, stop=True)
                ins.then_inc(p2v, 1)

            def bias(c):
                pe.wait_ge(v2p, c.next())
                for t in range(2):
                    for dw in range(3):
                        ins = nc.tensor.matmul(sm[2 * C * t:2 * C * (t + 1), 10:11], wn[:, dw], grp_i[:, 0:1],
                                               start=dw == 0, stop=dw == 2)
                ins.then_inc(p2v, 1)

            def conv_bank(n, u, h, g):
                b = (2 * h + g) % 4
                pe.wait_ge(evac, n * NGI + 2 * h + g + 1)
                k = HB * h + GK * g
                end = h == HC - 1 and g == 1
                copy_b = xb[h % 4][:, GK * g:GK * (g + 1)]
                for dw in range(3):
                    f = dict(start=dw == 0, stop=dw == 2)
                    ins = nc.tensor.matmul(cps[0:2 * C, b], wf[u][:, dw], xa[u][:, k:k + GK, dw:dw + W], **f)
                    if not end:
                        ins = nc.tensor.matmul(cps[2 * C:P, b], wf[u][:, dw], copy_b[:, :, dw:dw + W], **f)
                if end:
                    for dw in range(3):
                        nc.tensor.matmul(cps[2 * C:P, b, 0], wf[u][:, dw], copy_b[:, 0, dw:dw + W],
                                         start=dw == 0, stop=dw == 2)
                    for dw in range(3):
                        nc.tensor.matmul(cps[2 * C:3 * C, b, 1], wf[u][:, dw, 0], copy_b[:, 1, dw:dw + W],
                                         start=dw == 0, stop=dw == 2)
                    for dw in range(3):
                        ins = nc.tensor.matmul(cps[3 * C:P, b, 1], wf[u][:, dw, 1], xt[u][:, dw:dw + W],
                                               start=dw == 0, stop=dw == 2)
                ins.then_inc(conv_ready, 1)

            def turn_modes(n, u):
                pe.wait_ge(o1_loaded[u], (n - u) * 8 + 16)
                pe.wait_ge(y_added, n * NGI + 1)
                pe.sem_inc(passed, 1)
                for ky in range(M):
                    bank = yps[0:M, ky // 8].rearrange("p a b -> p (a b)")
                    ins = nc.tensor.transpose(bank[:, 64 * (ky % 8):64 * (ky % 8) + 64], o1[u][:, :, ky], ident[:])
                ins.then_inc(t_ready, 1)

            def row_spectra(n, half, q0):
                for q in range(q0, q0 + 2):
                    if q == 0:
                        pe.wait_ge(t_copied, n + 1)
                        pe.wait_ge(y_added, n * NGI + half * NGI // 2 + 1)
                    if q >= 3:
                        pe.wait_ge(g_copied, n * 16 + half * 8 + q - 2)
                    nc.tensor.matmul(yps[:, q % 3, 0, 0:H // 2], tt[:, 4 * q:4 * q + 4], eh[:, half * H // 2:(half + 1) * H // 2],
                                     start=True, stop=True).then_inc(g_ready, 1)

            def inverse_bank(n, g):
                if g % (NGI // 2) == 0:
                    pe.wait_ge(g_copied, n * 16 + 8 * (g // (NGI // 2)) + 8)
                if g >= 3:
                    pe.wait_ge(y_added, n * NGI + g - 1)
                for r in range(GK):
                    row = (GK * g + r) * S % (H // 2)
                    ins = nc.tensor.matmul(yps[:, g % 3, r], gs[:, row:row + S], ew[:], start=True, stop=True)
                ins.then_inc(y_ready, 1)

            pe.sem_inc(conv_ready, 8)
            pe.wait_ge(setup, N_SETUP)
            if not second:
                for t in range(9):
                    ins = nc.tensor.transpose(sm[0:C, C * t:C * (t + 1)], wraw[:, :, t // 3, t % 3], ident[:])
                ins.then_inc(turned, 1)
            pe.wait_ge(ready, 1)
            if second:
                turn_modes(0, 0)
                for half in range(2):
                    for q in range(0, 8, 2):
                        row_spectra(0, half, q)
                    for g in range(NGI // 2):
                        inverse_bank(0, NGI // 2 * half + g)
                turn_modes(1, 1)
            c = Count(0)
            input_mean(c)
            variance(c)
            if second:
                hidden(c)
                predicted(c)
            bias(c)

            def body(n, u, last, tail):
                c = Count(K_IN + n * K)
                for h in range(HC):
                    if h == 0:
                        pe.wait_ge(taps_ready, n + 1)
                        pe.wait_ge(xt_loaded[u], (n - u) * 8 + 16)
                    pe.wait_ge(xb_loaded[h % 4], n * 128 + (h // 4 + 1) * 32)
                    if second and not tail and h == 14:
                        turn_modes(n + 2, u)
                    for g in range(2):
                        if not last and (h, g) in spectra_at:
                            row_spectra(n + 1, *spectra_at[h, g])
                        conv_bank(n, u, h, g)
                        if (h, g) == (0, 1):
                            output_mean(c)
                        if (h, g) == (1, 0):
                            variance(c)
                        if last:
                            continue
                        if second:
                            for gg in range(banks_of[h] // 2):
                                inverse_bank(n + 1, starts[h] + banks_of[h] // 2 * g + gg)
                        if (h, g) == (13, 0):
                            input_mean(c)
                        if (h, g) == (13, 1):
                            variance(c)
                        if (h, g) == (14, 0) and second:
                            hidden(c)
                        if (h, g) == (14, 1) and second:
                            predicted(c)
                        if (h, g) == ((15, 0) if second else (14, 0)):
                            bias(c)
            image_loop(pe, body)
            c = Count(K_IN + (NB - 1) * K + 2)
            output_mean(c)
            variance(c)

        @block.scalar
        def _(act):
            def copy_modes(n):
                act.wait_ge(t_ready, n + 1)
                for b in range(2):
                    v = yps[0:M, b].rearrange("p a b -> p (a b)").rearrange("p (y r o) -> p r o y", r=2, o=C)
                    y = slice(8 * b, 8 * b + 8)
                    for r in range(2):
                        nc.scalar.activation(tt[0:M, :, r, y], v[:, r], ACT.Copy)
                    nc.scalar.activation(tt[C:C + M, :, 0, y], v[:, 1], ACT.Copy, scale=-1.0)
                    ins = nc.scalar.activation(tt[C:C + M, :, 1, y], v[:, 0], ACT.Copy)
                ins.then_inc(t_copied, 1)

            def copy_spectra(n, half, q0):
                for q in range(q0, q0 + 2):
                    act.wait_ge(g_ready, n * 16 + half * 8 + q + 1)
                    for o in range(4):
                        ins = nc.scalar.activation(gs[:, :, 4 * q + o], yps[C * o:C * (o + 1), q % 3, 0, 0:H // 2], ACT.Copy)
                    ins.then_inc(g_copied, 1)

            def root_of(n):
                act.wait_ge(var_ready, n + 1)
                nc.scalar.activation(root[:], veps[:], ACT.Sqrt).then_inc(root_ready, 1)

            act.dma_start(g8[:], const["g8"]).then_inc(setup, 16)
            act.dma_start(i3[:], const["i3"].rearrange("p (a b c) -> p a b c", a=3, b=2)).then_inc(setup, 16)
            n_id = 2 * C if second else C
            act.dma_start(ident[:], const["ident"][0:n_id, 0:n_id]).then_inc(setup, 16)
            if not second:
                act.dma_start(wraw[:], par["w"]).then_inc(setup, 16)
            else:
                act.dma_start(g4[:], const["g4"]).then_inc(setup, 16)
                act.dma_start(i4[:], const["i4"]).then_inc(setup, 16)
                act.dma_start(eh[:], const["eh"]).then_inc(setup, 16)
                act.dma_start(ew[:], const["ew"]).then_inc(setup, 16)
                act.dma_start(w1[:], par["w1"]).then_inc(setup, 16)
                act.dma_start(b1[:], par["b1"].rearrange("(a b) -> a b", b=1)).then_inc(setup, 16)
                act.dma_start(w2raw[:], par["w2"].rearrange("p (c h w) -> p c h w", h=3, w=3)).then_inc(setup, 16)
                act.dma_start(mpad[:], const["ones"][:, 0:PAD]).then_inc(setup, 16)
                act.dma_start(b2c[:], par["b2"].rearrange("(c h w) -> c h w", h=3, w=3)).then_inc(setup, 16)
            act.sem_inc(evac, 4)
            act.wait_ge(ready, 1)
            if second:
                copy_modes(0)
                for half in range(2):
                    for q in range(0, 8, 2):
                        copy_spectra(0, half, q)
                copy_modes(1)
            root_of(0)

            def body(n, u, last, tail):
                act.wait_ge(nb_ready, n + 1)
                for h in range(HC):
                    o = h % 4
                    act.wait_ge(stored[o], n * 16 * (4 * S + (o == 3)) + 16 * S * (h // 4) + 1)
                    act.wait_ge(ostat, n * HC + h + 1)
                    if second and not tail and h == 14:
                        copy_modes(n + 2)
                    for g in range(2):
                        if not last and (h, g) in spectra_at:
                            copy_spectra(n + 1, *spectra_at[h, g])
                        act.wait_ge(conv_ready, n * NGI + 8 + 2 * h + g + 1)
                        nc.scalar.activation(oc[o][:, GK * g:GK * (g + 1)], cps[:, (2 * h + g) % 4], ACT.Identity,
                                             bias=nb[u][:, 0:1]).then_inc(evac, 1)
                    if h == 13 and not last:
                        root_of(n + 1)
            image_loop(act, body)

        @block.vector
        def _(dve):
            v = nc.vector

            def chained(c, ins):
                ins.then_inc(link, 1)
                dve.wait_ge(link, c.next())

            c = Count(0)
            dve.sem_inc(ostat, 4)
            dve.sem_inc(y_added, 1)
            v.memset(ones[:], 1.0)
            v.memset(ost[:], 1.0)
            for u in range(2):
                v.memset(xa[u][2 * C:P, KB, :], 0.0)
            if not second:
                chained(c, v.memset(wb[:], 0.0))
                dve.wait_ge(turned, 1)
                w = sm[0:C, 0:9 * C].rearrange("p (h w o) -> p h w o", h=3, w=3)
                for i in range(2):
                    for kh in range(3):
                        j = i + kh
                        ins = v.tensor_scalar(wb[C * j:C * (j + 1), :, i, :], w[:, kh], 0.0, 2.0 / DIV, ALU.is_gt, ALU.mult)
                chained(c, ins)
                for i in range(2):
                    for kh in range(3):
                        j = i + kh
                        cells = wb[C * j:C * (j + 1), :, i, :]
                        ins = v.tensor_scalar(cells, cells, -1.0 / DIV, None, ALU.add)
                chained(c, ins)
            else:
                v.memset(b2r[:], 0.0)
                v.memset(tt[:], 0.0)
                chained(c, v.memset(w2r[:], 0.0))
                dve.wait_ge(setup, N_SETUP)
                for i in range(2):
                    for kh in range(3):
                        for kw in range(3):
                            v.tensor_copy(w2r[:, kw, i, i + kh, :], w2raw[:, :, kh, kw])
                        j = i + kh
                        ins = v.tensor_copy(b2r[C * j:C * (j + 1), :, i], b2c[:, kh, :])
                chained(c, ins)
            dve.sem_inc(ready, 1)
            dve.wait_ge(setup, N_SETUP)

            def input_banks(n, u, g0, g1):
                for g in range(g0, g1):
                    cells = xa[u][:, GK * g:GK * (g + 1), 1:W + 1]
                    if g % (2 * NG) == 0:
                        dve.wait_ge(xa_loaded[u][g // (2 * NG)], (n - u) * 64 + 128)
                    if second:
                        dve.wait_ge(y_ready, n * NGI + g + 1)
                        v.tensor_tensor(cells, cells, yps[:, g % 3], ALU.add).then_inc(y_added, 1)
                        dve.wait_ge(y_added, n * NGI + g + 2)
                    ins = v.bn_stats(ist[:, g, :], cells)
                    if g == NGI - 1:
                        ins.then_inc(istat, 1)

            def mean(c, cp, agg, st, grp):
                v.bn_aggr(agg[:], st[:].rearrange("p g s -> p (g s)")).then_inc(v2p, 1)
                dve.wait_ge(p2v, cp.next())
                v.tensor_copy(grp[:, 0:1], sm[:, 0:1])
                chained(c, v.tensor_tensor(dev[:], agg[:, 0:1], sm[:, 0:1], ALU.subtract))
                v.scalar_tensor_tensor(out=var[:], in0=dev[:], scalar=dev[:, 0:1], in1=agg[:, 1:2],
                                       op0=ALU.mult, op1=ALU.add).then_inc(v2p, 1)

            def input_norm(c, cp, n, u):
                dve.wait_ge(istat, n + 1)
                dve.sem_inc(passed, 1)
                mean(c, cp, agg_i, ist, grp_i)
                v.tensor_scalar(xa[u][:, 0:KB, 0:W + 2:W + 1], ones[:, 0:2 * KB].rearrange("p (a b) -> p a b", b=2),
                                grp_i[:, 0:1], None, ALU.mult)
                v.tensor_scalar(xt[u][0:2 * C, :], ones[0:2 * C, :], grp_i[0:2 * C, 0:1], None, ALU.mult)
                v.tensor_scalar(xa[u][0:2 * C, KB, :], ones[0:2 * C, :], grp_i[0:2 * C, 0:1], None,
                                ALU.mult).then_inc(xa_final, 1)
                dve.wait_ge(p2v, cp.next())
                chained(c, v.tensor_scalar(veps[:], sm[:, 1:2], EPS, None, ALU.add))
                dve.sem_inc(var_ready, 1)
                dve.wait_ge(root_ready, n + 1)
                chained(c, v.reciprocal(inv[:], root[:]))
                chained(c, v.scalar_tensor_tensor(out=half[:], in0=inv[:], scalar=inv[:, 0:1], in1=veps[:],
                                                  op0=ALU.mult, op1=ALU.mult))
                chained(c, v.tensor_scalar(half[:], half[:], -0.5, 1.5, ALU.mult, ALU.add))
                chained(c, v.tensor_tensor(scl[:], inv[:], half[:], ALU.mult))
                if second:
                    v.tensor_scalar(pool[:], sm[:, 2:3], grp_i[:, 0:1], scl[:, 0:1], ALU.subtract, ALU.mult).then_inc(v2p, 1)
                else:
                    v.tensor_scalar(wn[:], wb[:], scl[:, 0:1], None, ALU.mult).then_inc(v2p, 1)

            def predict(c, cp):
                dve.wait_ge(p2v, cp.next())
                v.tensor_scalar(hdn[:], sm[:, 3:4], b1[:, 0:1], 0.0, ALU.add, ALU.max).then_inc(v2p, 1)
                dve.wait_ge(p2v, cp.next())
                chained(c, v.tensor_tensor(kern[:], sm[:, 4:10], b2r[:].rearrange("p a b -> p (a b)"), ALU.add))
                chained(c, v.tensor_scalar(kn[:], kern[:], scl[:, 0:1], None, ALU.mult))
                taps6 = wn[:].rearrange("p a b o -> p (a b) o")
                for t in range(6):
                    ins = v.tensor_scalar(taps6[:, t, :], i4[:], kn[:, t:t + 1], None, ALU.mult)
                ins.then_inc(v2p, 1)

            def taps(cp, u):
                dve.wait_ge(p2v, cp.next())
                v.tensor_tensor(wf[u][:], wn[:], i3[:], ALU.add).then_inc(taps_ready, 1)
                v.tensor_scalar(nb[u][:], sm[:, 10:11], -1.0, None, ALU.mult).then_inc(nb_ready, 1)

            def output_norm(c, cp, n):
                dve.wait_ge(ostat, n * HC + 4)
                dve.wait_ge(grp_stored, n * 16 * (1 + S * second) + 1)
                dve.sem_inc(passed, 1)
                mean(c, cp, agg_o, ost, grp_o)
                dve.wait_ge(p2v, cp.next())
                chained(c, v.tensor_copy(grp_o[:, 1:2], sm[:, 1:2]))
                if second:
                    v.tensor_scalar(mpads[:], mpad[:].unsqueeze(1).broadcast_to([P, KB, PAD]), grp_o[:, 0:1],
                                    None, ALU.mult).then_inc(grp_ready, 1)
                else:
                    dve.sem_inc(grp_ready, 1)

            input_banks(0, 0, 0, NGI)
            cp = Count(0)
            input_norm(c, cp, 0, 0)
            if second:
                predict(c, cp)
            taps(cp, 0)
            c0 = c.n
            links = 10 if second else 8

            def body(n, u, last, tail):
                c, cp = Count(c0 + n * links), Count(K_IN + n * K)
                output_norm(c, cp, n)
                for h in range(HC):
                    if not last:
                        input_banks(n + 1, 1 - u, starts[h], starts[h] + banks_of[h])
                        if h == 13:
                            input_norm(c, cp, n + 1, 1 - u)
                        if h == 14 and second:
                            predict(c, cp)
                        if h == (15 if second else 14):
                            taps(cp, 1 - u)
                    dve.wait_ge(evac, n * NGI + 4 + 2 * (h + 1))
                    for g in range(2):
                        ins = v.bn_stats(ost[:, 2 * h + g, :], oc[h % 4][:, GK * g:GK * (g + 1)])
                    ins.then_inc(ostat, 1)
                assert last or c.n == links, c.n
            image_loop(dve, body)
            output_norm(Count(c0 + (NB - 1) * links + 2), Count(K_IN + (NB - 1) * K + 2), NB)


def spectrum_phase(nc, src, spectra, const):
    with ExitStack() as ctx:
        def sb(name, shape):
            return ctx.enter_context(nc.sbuf_tensor(f"{name}_sp", shape, F32))

        def sem(name):
            return ctx.enter_context(nc.semaphore(f"{name}_sp"))

        xh = [sb(f"xh{u}", [P, 2, C, W]) for u in range(2)]
        col = sb("col", [P, 4, 2 * W])
        turn = sb("turn", [P, 2, 8, P])
        xs = [sb(f"xs{u}", [2 * C, M, M]) for u in range(2)]
        fh = sb("fh", [P, 2, 2 * M])
        fw = sb("fw", [P, 2, 2, 2 * M])
        ident = sb("ident", [P, P])
        cp_ = ctx.enter_context(nc.psum_tensor("cp_sp", [P, 4, 512], F32))
        tp = ctx.enter_context(nc.psum_tensor("tp_sp", [P, 4, 4, P], F32))

        setup = sem("setup")
        loaded = [sem(f"loaded{u}") for u in range(2)]
        col_ready = sem("col_ready")
        col_act = sem("col_act")
        col_dve = sem("col_dve")
        turn_ready = sem("turn_ready")
        turn_act = sem("turn_act")
        turn_dve = sem("turn_dve")
        modes_ready = sem("modes_ready")
        modes_act = sem("modes_act")
        modes_dve = sem("modes_dve")
        stored = [sem(f"stored{u}") for u in range(2)]

        block = ctx.enter_context(nc.Block(name="spectrum"))

        def load_image(eng, n, u):
            for half in range(2):
                rows = image(src, n).rearrange("b c (f p) w -> f p (b c) w", f=2)[half]
                eng.dma_start(xh[u][:, half], rows).then_inc(loaded[u], 16)

        @block.sync
        def _(sp):
            for u in range(2):
                sp.sem_inc(stored[u], 1)
            load_image(sp, 0, 0)
            sp.dma_start(fh[:], const["fh"].rearrange("p (a b) -> p a b", a=2)).then_inc(setup, 16)
            sp.dma_start(fw[:], const["fw"].rearrange("p (a b c) -> p a b c", a=2, b=2)).then_inc(setup, 16)
            sp.dma_start(ident[:], const["ident"]).then_inc(setup, 16)
            load_image(sp, 1, 1)

            def body(n, u, last, tail):
                if not tail:
                    sp.wait_ge(col_ready, (n + 1) * 4)
                    load_image(sp, n + 2, u)
                sp.wait_ge(modes_act, n + 2)
                sp.wait_ge(modes_dve, n + 2)
                sp.dma_start(image(spectra, n).rearrange("b p (x y) -> (b p) x y", y=M), xs[u][:]).then_inc(stored[u], 16)
            image_loop(sp, body)
            for u in range(2):
                sp.wait_ge(stored[u], NB // 2 * 16 + 1)

        @block.tensor
        def _(pe):
            pe.wait_ge(setup, 48)

            def body(n, u, last, tail):
                pe.wait_ge(loaded[u], (n - u) * 16 + 32)
                pe.wait_ge(modes_act, n + 1)
                pe.wait_ge(modes_dve, n + 1)
                for nb in range(4):
                    for q in range(4):
                        for half in range(2):
                            first = 8 * nb + q
                            ins = nc.tensor.matmul(cp_[C * q:C * (q + 1), nb], fh[:, half], xh[u][:, half, first:first + 5:4, :],
                                                   start=half == 0, stop=half == 1)
                    ins.then_inc(col_ready, 1)
                for half in range(2):
                    for j in range(8):
                        if half == 0 and j == 0:
                            pe.wait_ge(col_act, 2 * n + 2)
                            pe.wait_ge(turn_act, 2 * n + 1)
                            pe.wait_ge(turn_dve, 2 * n + 1)
                        if half == 0 and j == 4:
                            pe.wait_ge(col_dve, 2 * n + 2)
                        at = (j % 2) * W + half * P
                        ins = nc.tensor.transpose(tp[:, 2 * half + j // 4, j % 4], col[:, j // 2, at:at + P], ident[:])
                        if j % 4 == 3:
                            ins.then_inc(turn_ready, 1)
                for kx in range(M):
                    for half in range(2):
                        if kx == 0:
                            pe.wait_ge(turn_act if half == 0 else turn_dve, 2 * n + 3)
                        for r in range(2):
                            lhs = turn[:, half].rearrange("p j (q r k) -> p (j q) (r k)", q=4, r=2)[:, :, r * M + kx]
                            ins = nc.tensor.matmul(cp_[0:C, 0, 2 * M * kx:2 * M * (kx + 1)], lhs, fw[:, half, r],
                                                   start=half == 0 and r == 0, stop=half == 1 and r == 1)
                ins.then_inc(modes_ready, 1)
            image_loop(pe, body)

        def evacuate(eng, copy, mine, col_done, turn_done, modes_done):
            eng.sem_inc(turn_done, 1)
            eng.sem_inc(modes_done, 1)

            def body(n, u, last, tail):
                for k in range(2):
                    nb = 2 * mine + k
                    eng.wait_ge(col_ready, 4 * n + nb + 1)
                    copy(col[:, nb], cp_[:, nb]).then_inc(col_done, 1)
                for k in range(2):
                    eng.wait_ge(turn_ready, 4 * n + 2 * mine + k + 1)
                    copy(turn[:, mine, 4 * k:4 * k + 4], tp[:, 2 * mine + k]).then_inc(turn_done, 1)
                if mine:
                    eng.wait_ge(modes_act, n + 2)
                eng.wait_ge(modes_ready, n + 1)
                eng.wait_ge(stored[u], (n - u) * 8 + 1)
                modes = cp_[0:C, 0].rearrange("p (x r y) -> p r x y", r=2, y=M)
                copy(xs[u][C * mine:C * (mine + 1)], modes[:, mine]).then_inc(modes_done, 1)
            image_loop(eng, body)

        @block.scalar
        def _(act):
            evacuate(act, lambda o, i: nc.scalar.activation(o, i, ACT.Copy), 0, col_act, turn_act, modes_act)

        @block.vector
        def _(dve):
            evacuate(dve, lambda o, i: nc.vector.tensor_copy(o, i), 1, col_dve, turn_dve, modes_dve)


def mixing_phase(nc, spectra, stats, weights, mixed):
    with ExitStack() as ctx:
        def sb(name, shape):
            return ctx.enter_context(nc.sbuf_tensor(f"{name}_mx", shape, F32))

        def sem(name):
            return ctx.enter_context(nc.semaphore(f"{name}_mx"))

        wm = sb("wm", [2 * C, C, MM, 2])
        wr = sb("wr", [2 * C, C, MM, 2])
        x = sb("x", [2 * C, NB, MM])
        o = sb("o", [2 * C, NB, MM])
        st = sb("st", [2 * C, NB, 2])
        veps, root, inv, half, scl = (sb(n, [2 * C, NB]) for n in ("veps", "root", "inv", "half", "scl"))
        ps = ctx.enter_context(nc.psum_tensor("ps_mx", [2 * C, 8, 32, 16], F32))
        loaded = sem("loaded")
        w_loaded = [sem(f"w_loaded{k}") for k in range(4)]
        link = sem("link")
        root_ready = sem("root_ready")
        x_ready = sem("x_ready")
        w_act = sem("w_act")
        w_dve = sem("w_dve")
        ready = sem("ready")
        o_act = sem("o_act")
        o_dve = sem("o_dve")
        stored = sem("stored")
        block = ctx.enter_context(nc.Block(name="mixing"))

        def modes(k):
            return slice(MM // 4 * k, MM // 4 * (k + 1))

        @block.sync
        def _(sp):
            sp.dma_start(x[:], spectra.rearrange("b p m -> p b m")).then_inc(loaded, 16)
            for r in range(2):
                sp.dma_start(st[C * r:C * (r + 1)], stats.rearrange("b c s -> c b s")).then_inc(loaded, 16)
            w = weights.rearrange("i o x y r -> i o (x y) r")
            for k in range(4):
                sp.dma_start(wr[C:2 * C, :, modes(k)], w[:, :, modes(k)]).then_inc(w_loaded[k], 16)
                sp.dma_start(wm[0:C, :, modes(k)], w[:, :, modes(k)]).then_inc(w_loaded[k], 16)
            sp.wait_ge(o_act, 4)
            sp.wait_ge(o_dve, 4)
            sp.dma_start(mixed.rearrange("b p m -> p b m"), o[:]).then_inc(stored, 16)
            sp.wait_ge(stored, 16)

        @block.vector
        def _(dve):
            v = nc.vector
            dve.wait_ge(loaded, 48)
            v.tensor_scalar(veps[:], st[:, :, 1], EPS, None, ALU.add).then_inc(link, 1)
            v.scalar_tensor_tensor(out=x[0:C, :, 0], in0=st[0:C, :, 0], scalar=-float(H * W), in1=x[0:C, :, 0],
                                   op0=ALU.mult, op1=ALU.add)
            dve.wait_ge(root_ready, 1)
            v.reciprocal(inv[:], root[:]).then_inc(link, 1)
            dve.wait_ge(link, 2)
            v.tensor_tensor(half[:], inv[:], inv[:], ALU.mult).then_inc(link, 1)
            dve.wait_ge(link, 3)
            v.tensor_tensor(half[:], half[:], veps[:], ALU.mult).then_inc(link, 1)
            dve.wait_ge(link, 4)
            v.tensor_scalar(half[:], half[:], -0.5, 1.5, ALU.mult, ALU.add).then_inc(link, 1)
            dve.wait_ge(link, 5)
            v.tensor_tensor(scl[:], inv[:], half[:], ALU.mult).then_inc(link, 1)
            dve.wait_ge(link, 6)
            v.tensor_tensor(x[:], x[:], scl[:].unsqueeze(2).broadcast_to([2 * C, NB, MM]), ALU.mult).then_inc(x_ready, 1)
            for k in range(4):
                dve.wait_ge(w_loaded[k], 32)
                v.tensor_copy(wm[C:2 * C, :, modes(k), 1], wr[C:2 * C, :, modes(k), 0]).then_inc(w_dve, 1)
            for k in range(1, 8, 2):
                dve.wait_ge(ready, k + 1)
                v.tensor_copy(o[:, :, 32 * k:32 * k + 32], ps[:, k, :, 0:NB].rearrange("p m b -> p b m")).then_inc(o_dve, 1)

        @block.scalar
        def _(act):
            act.wait_ge(link, 1)
            nc.scalar.activation(root[:], veps[:], ACT.Sqrt).then_inc(root_ready, 1)
            for k in range(4):
                act.wait_ge(w_loaded[k], 32)
                nc.scalar.activation(wm[C:2 * C, :, modes(k), 0], wr[C:2 * C, :, modes(k), 1], ACT.Copy, scale=-1.0).then_inc(w_act, 1)
            for k in range(0, 8, 2):
                act.wait_ge(ready, k + 1)
                nc.scalar.activation(o[:, :, 32 * k:32 * k + 32], ps[:, k, :, 0:NB].rearrange("p m b -> p b m"), ACT.Copy).then_inc(o_act, 1)

        @block.tensor
        def _(pe):
            pe.wait_ge(x_ready, 1)
            for m in range(MM):
                if m % (MM // 4) == 0:
                    pe.wait_ge(w_act, m // (MM // 4) + 1)
                    pe.wait_ge(w_dve, m // (MM // 4) + 1)
                for r in range(2):
                    ins = nc.tensor.matmul(ps[C * r:C * (r + 1), m // 32, m % 32, 0:NB], wm[:, :, m, r], x[:, :, m],
                                           start=True, stop=True)
                if m % 32 == 31:
                    ins.then_inc(ready, 1)


GH = 2
GB = S
STEPS = W
BLOCKS = STEPS // T
EARLY = 4
OUT, FORGET, IN, CELL = range(4)


def lstm_phase(nc, src, out, stats, par, const):
    with ExitStack() as ctx:
        def sb(name, shape):
            return ctx.enter_context(nc.sbuf_tensor(f"{name}_ls", shape, F32))

        def sem(name):
            return ctx.enter_context(nc.semaphore(f"{name}_ls"))

        def sems(name):
            return [sem(f"{name}{k}") for k in range(2)]

        xs = [sb(f"xs{k}", [P, GH, H, T + 1]) for k in range(2)]
        ys = [sb(f"ys{k}", [P, GH, H, T]) for k in range(2)]
        stack = sb("stack", [P, 2, GH, 2, H + 1])
        hid = sb("hid", [P, 2, GH, H])
        cell = sb("cell", [P, GH, H])
        gate = sb("gate", [P, GH, 4, H])
        w1d = gate[:, 0].rearrange("p k (j o) -> p j k o", j=2)
        fc, ig, tc = (sb(n, [P, GH, H]) for n in ("fc", "ig", "tc"))
        below = sb("below", [P, GH, STEPS - T])
        band = sb("band", [P, GH, T, STEPS - T])
        w2d = sb("w2d", [P, 4, P])
        own = sb("own", [P, 2, 4, 2 * C])
        above = sb("above", [P, 2, 4, 2 * C])
        w2raw = sb("w2raw", [P, C])
        w1raw = sb("w1raw", [P, C, 2])
        b1row, b2row, brow = (sb(n, [4, C]) for n in ("b1row", "b2row", "brow"))
        b12 = sb("b12", [P, 4])
        mean = sb("mean", [P, GH])
        st = sb("st", [P, GH, 2])
        veps, root, inv, half, scl = (sb(n, [P, GH]) for n in ("veps", "root", "inv", "half", "scl"))
        ident = sb("ident", [P, P])
        ps = ctx.enter_context(nc.psum_tensor("ps_ls", [P, GH, 4, 512], F32))
        small = ps[:, 0, 0]

        setup = sem("setup")
        passed = sem("passed")
        turned = sem("turned")
        ready = sem("ready")
        zeroed = sem("zeroed")
        link = sem("link")
        st_loaded = sem("st_loaded")
        root_ready = sem("root_ready")
        veps_ready = sem("veps_ready")
        scl_ready = sem("scl_ready")
        norm_ready = sem("norm_ready")
        xs_loaded, ys_loaded, ys_stored = sems("xs_loaded"), sems("ys_loaded"), sems("ys_stored")
        sums_ready = sems("sums_ready")
        gates_ready = sems("gates_ready")
        parts_ready = sems("parts_ready")
        cell_ready = sems("cell_ready")
        tanh_ready = sems("tanh_ready")
        stack_ready = sems("stack_ready")
        hid_ready = sems("hid_ready")
        added = sems("added")
        band_loaded, band_stored = sems("band_loaded"), sems("band_stored")

        rows_of = [min(H, T * (tb + 1) + 1) for tb in range(BLOCKS)]
        order = (FORGET, IN, CELL, OUT)
        pairs = [slice(2 * C * j, 2 * C * (j + 1)) for j in range(2)]
        hidden_at = [pairs[1], pairs[0]]

        def steps(eng, hf, tb, body, first=0, end=T):
            eng.sem_inc(passed, 1)
            with eng.Fori(first // 2, end // 2) as i:
                for parity in range(2):
                    body(2 * i + parity, parity)

        def early_of(g):
            return g * EARLY

        def at(hf, g, steps_done):
            return hf * (STEPS - T * early_of(g)) + (steps_done - T * early_of(g))

        def stacks(hf, g, tb, steps_done):
            return hf * (BLOCKS - early_of(g)) + (at(hf, g, steps_done) + (2 + tb - early_of(g)))

        def groups_in(tb):
            return range(1 if tb < EARLY else GH)

        def cells_in(tb, g):
            return slice(0, GH) if tb < EARLY else slice(g, g + 1)

        def sums(tb, g, parity):
            n = rows_of[tb]
            if tb < EARLY:
                return ps[:, parity].rearrange("p k (g h) -> p k g h", g=GH)[:, :, :, 0:n]
            return ps[:, g].rearrange("p k (g h) -> p k g h", g=GH)[:, :, 0:1, 0:n]

        def groups_of(t, hf, g):
            return t[bass.ds(hf * (GH * GB) + GB * g, GB)]

        block = ctx.enter_context(nc.Block(name="lstm"))

        @block.sync
        def _(sp):
            for p in range(2):
                sp.sem_inc(ys_stored[p], 1)
                sp.sem_inc(band_stored[p], 1)
            sp.dma_start(ident[:], const["ident"]).then_inc(setup, 16)
            sp.dma_start(w2raw[:], par["W2"]).then_inc(setup, 16)
            sp.dma_start(w1raw[:], par["W1"]).then_inc(setup, 16)
            sp.dma_start(b1row[:], par["b1"].rearrange("(k o) -> k o", k=4)).then_inc(setup, 16)
            sp.dma_start(b2row[:], par["b2"].rearrange("(k o) -> k o", k=4)).then_inc(setup, 16)

            def load_stats(of):
                for g in range(GH):
                    sp.dma_start(st[:, g], groups_of(stats, of, g).rearrange("b c s -> (b c) s")).then_inc(st_loaded, 16)

            def load(of, tb, ys_free):
                p, n, t0 = tb % 2, rows_of[tb], T * tb
                for g in range(GH):
                    skewed = groups_of(src, of, g).rearrange("b c h w -> (b c) (h w)")[:, PAD + t0:PAD + t0 + n * (WX - 1)]
                    sp.dma_start(xs[p][:, g, 0:n, :], skewed.rearrange("p (h w) -> p h w", w=WX - 1)[:, :, 0:T + 1]).then_inc(xs_loaded[p], 16)
                ys_free()
                for g in range(GH):
                    cells = groups_of(src, of, g).rearrange("b c h w -> (b c) h w")[:, 0:t0 + T, PAD + t0:PAD + t0 + T]
                    sp.dma_start(ys[p][:, g, 0:t0 + T], cells).then_inc(ys_loaded[p], 16)

            load_stats(0)
            load(0, 0, lambda: None)
            with sp.Fori(0, 2) as hf:
                other = hf * -1 + 1

                def load_next(tb):
                    if tb >= 2:
                        for g in groups_in(tb - 2):
                            sp.wait_ge(stack_ready[g], stacks(hf, g, tb - 2, T * (tb - 1)))
                            sp.sem_inc(passed, 1)
                    else:
                        for g in range(GH):
                            sp.wait_ge(stack_ready[g], stacks(hf, g, early_of(g), T * early_of(g)) - 1)
                            sp.sem_inc(passed, 1)
                    if tb == BLOCKS:
                        sp.wait_ge(norm_ready, hf + 1)
                    sp.sem_inc(passed, 1)
                    if tb == BLOCKS:
                        load_stats(other)

                    def ys_free():
                        sp.wait_ge(ys_stored[tb % 2], (hf * (BLOCKS // 2) + tb // 2) * 32 + 1)
                        sp.sem_inc(passed, 1)
                    if tb < BLOCKS:
                        load(hf, tb, ys_free)
                    else:
                        load(other, 0, ys_free)

                def load_band(tb, b):
                    rows = slice(T * tb + T // 2 * b, T * tb + T // 2 * (b + 1))
                    sp.wait_ge(band_stored[b], (hf * (BLOCKS - 1) + (tb - 1)) * 32 + 1)
                    for g in range(GH):
                        cells = groups_of(src, hf, g).rearrange("b c h w -> (b c) h w")[:, rows, PAD:PAD + T * tb]
                        sp.dma_start(band[:, g, T // 2 * b:T // 2 * (b + 1), 0:T * tb], cells).then_inc(band_loaded[b], 16)

                def store_band(tb, b):
                    rows = slice(T * tb + T // 2 * b, T * tb + T // 2 * (b + 1))
                    for g in range(GH):
                        if g in groups_in(tb):
                            sp.wait_ge(added[g], at(hf, g, T * tb + T // 2 * (b + 1)) + 2)
                        cells = groups_of(out, hf, g).rearrange("b c h w -> (b c) h w")[:, rows, 0:T * tb]
                        sp.dma_start(cells, band[:, g, T // 2 * b:T // 2 * (b + 1), 0:T * tb]).then_inc(band_stored[b], 16)

                for tb in range(BLOCKS):
                    load_next(tb + 1)
                    if tb:
                        store_band(tb, 0)
                    if tb + 1 < BLOCKS:
                        load_band(tb + 1, 0)
                    for g in range(GH):
                        if g in groups_in(tb):
                            sp.wait_ge(added[g], at(hf, g, T * (tb + 1)) + 2)
                        cells = groups_of(out, hf, g).rearrange("b c h w -> (b c) h w")[:, 0:T * (tb + 1), T * tb:T * (tb + 1)]
                        sp.dma_start(cells, ys[tb % 2][:, g, 0:T * (tb + 1)]).then_inc(ys_stored[tb % 2], 16)
                    if tb:
                        store_band(tb, 1)
                    if tb + 1 < BLOCKS:
                        load_band(tb + 1, 1)
            sp.wait_ge(st_loaded, 3 * 32)
            sp.wait_ge(xs_loaded[0], (BLOCKS + 1) * 32)
            sp.wait_ge(ys_loaded[0], (BLOCKS + 1) * 32)
            for p in range(2):
                sp.wait_ge(ys_stored[p], BLOCKS * 32 + 1)
                sp.wait_ge(band_stored[p], 2 * (BLOCKS - 1) * 32 + 1)

        @block.tensor
        def _(pe):
            pe.wait_ge(setup, 80)
            pe.wait_ge(link, 1)
            nc.tensor.transpose(small[0:C, 0:P], w2raw[:], ident[:])
            for j in range(2):
                nc.tensor.transpose(small[0:C, P * (1 + j):P * (2 + j)], w1raw[:, :, j], ident[:])
            nc.tensor.transpose(ps[0:C, 1, 0, 0:4], brow[:], ident[0:4, 0:4]).then_inc(turned, 1)
            pe.wait_ge(ready, 1)

            with pe.Fori(0, 2) as hf:
                for tb in range(BLOCKS):
                    n = rows_of[tb]

                    def step(tau, parity):
                        for g in groups_in(tb):
                            pe.wait_ge(stack_ready[g], stacks(hf, g, tb, T * tb) + tau)
                            to = sums(tb, g, parity)
                            for k in order:
                                for j in range(2):
                                    x = stack[:, parity, cells_in(tb, g), j]
                                    nc.tensor.matmul(to[pairs[j], k], own[:, j, k], x[:, :, 1:n + 1], start=True, stop=False)
                                    ins = nc.tensor.matmul(to[pairs[j], k], above[:, j, k], x[:, :, 0:n], start=False, stop=True)
                                ins.then_inc(sums_ready[g], 1)
                    steps(pe, hf, tb, step)

        @block.scalar
        def _(act):
            with act.Fori(0, 2) as hf:
                act.wait_ge(veps_ready, hf + 1)
                nc.scalar.activation(root[:], veps[:], ACT.Sqrt).then_inc(root_ready, 1)
                for tb in range(BLOCKS):
                    n = rows_of[tb]

                    def step(tau, parity):
                        for g in groups_in(tb):
                            gs, to, done = cells_in(tb, g), sums(tb, g, parity), at(hf, g, T * tb) + tau
                            for nth, k in enumerate(order):
                                act.wait_ge(sums_ready[g], done * 4 + (nth + 1))
                                if k == OUT:
                                    act.wait_ge(hid_ready[g], done + 1)
                                f = ACT.Tanh if k == CELL else ACT.Sigmoid
                                nc.scalar.activation(gate[:, gs, k, 0:n], to[:, k], f,
                                                     bias=b12[:, k:k + 1]).then_inc(gates_ready[g], 1)
                            act.wait_ge(cell_ready[g], done + 1)
                            nc.scalar.activation(tc[:, gs, 0:n], cell[:, gs, 0:n], ACT.Tanh).then_inc(tanh_ready[g], 1)
                    steps(act, hf, tb, step)

        @block.vector
        def _(dve):
            v = nc.vector
            for g in range(GH):
                dve.sem_inc(stack_ready[g], 1)
                dve.sem_inc(hid_ready[g], 1)
            v.memset(w2d[:], 0.0)
            v.memset(gate[:, 0], 0.0)
            v.memset(above[:], 0.0)
            dve.wait_ge(setup, 80)
            v.tensor_tensor(brow[:], b1row[:], b2row[:], ALU.add).then_inc(link, 1)
            dve.wait_ge(link, 1)
            dve.wait_ge(turned, 1)
            for q in range(GB):
                here = slice(C * q, C * (q + 1))
                v.tensor_copy(w2d[here, :, here], small[0:C, 0:P].rearrange("p (k o) -> p k o", k=4))
                for j in range(2):
                    v.tensor_copy(w1d[here, j, :, here], small[0:C, P * (1 + j):P * (2 + j)].rearrange("p (k o) -> p k o", k=4))
                ins = v.tensor_copy(b12[here, :], ps[0:C, 1, 0, 0:4])
            ins.then_inc(ready, 1)
            dve.wait_ge(ready, 1)
            for j in range(2):
                v.tensor_copy(above[hidden_at[j], j], w1d[pairs[j], 0, :, pairs[j]])
                v.tensor_copy(own[pairs[j], j], w2d[pairs[j], :, pairs[j]])
                ins = v.tensor_copy(own[hidden_at[j], j], w1d[pairs[j], 1, :, pairs[j]])
            ins.then_inc(ready, 1)
            dve.wait_ge(ready, 2)

            with dve.Fori(0, 2) as hf:
                c = Count(hf * 5 + 1)

                def chained(ins):
                    ins.then_inc(link, 1)
                    dve.wait_ge(link, c.next())

                dve.wait_ge(st_loaded, hf * 32 + 32)
                chained(v.tensor_scalar(veps[:], st[:, :, 1], EPS, None, ALU.add))
                dve.sem_inc(veps_ready, 1)
                dve.wait_ge(root_ready, hf + 1)
                chained(v.reciprocal(inv[:], root[:]))
                chained(v.tensor_tensor(half[:], inv[:], inv[:], ALU.mult))
                chained(v.tensor_tensor(half[:], half[:], veps[:], ALU.mult))
                chained(v.tensor_scalar(half[:], half[:], -0.5, 1.5, ALU.mult, ALU.add))
                v.tensor_tensor(scl[:], inv[:], half[:], ALU.mult).then_inc(scl_ready, 1)
                dve.wait_ge(scl_ready, hf + 1)
                v.tensor_copy(mean[:], st[:, :, 0]).then_inc(norm_ready, 1)
                dve.wait_ge(norm_ready, hf + 1)
                dve.wait_ge(added[1], at(hf, 1, T * EARLY) + 2)
                dve.sem_inc(passed, 1)
                v.memset(cell[:], 0.0)
                v.memset(stack[:], 0.0).then_inc(zeroed, 1)
                dve.wait_ge(zeroed, hf + 1)
                def norm(p, parity, g, j, rows, tau):
                    h = pairs[j]
                    return v.tensor_scalar(stack[h, parity, g, j, rows.start + 1:rows.stop + 1],
                                           xs[p][h, g, rows, bass.ds(tau, 1)].rearrange("p h t -> p (h t)"),
                                           mean[h, g:g + 1], scl[h, g:g + 1], ALU.subtract, ALU.mult)

                def start_block(tb, g):
                    n, p, gs = rows_of[tb], tb % 2, cells_in(tb, g)
                    m = rows_of[tb - 1] if tb else 0
                    dve.wait_ge(xs_loaded[p], (hf * (BLOCKS // 2) + tb // 2 + 1) * 32)
                    dve.sem_inc(passed, 1)
                    if tb:
                        if g in groups_in(tb - 1):
                            dve.wait_ge(stack_ready[g], stacks(hf, g, tb - 1, T * tb))
                        wide = [P, gs.stop - gs.start, n - m]
                        v.tensor_copy(cell[:, gs, m:n], cell[:, gs, m - 1:m].broadcast_to(wide))
                        for j in range(2):
                            h = stack[hidden_at[j], 0, gs, j]
                            v.tensor_copy(h[:, :, m + 1:n + 1], h[:, :, m:m + 1].broadcast_to([2 * C] + wide[1:]))
                    for each in range(gs.start, gs.stop):
                        for j in range(2):
                            ins = norm(p, 0, each, j, slice(m, n), 0)
                    ins.then_inc(stack_ready[g], 1)
                    dve.wait_ge(stack_ready[g], stacks(hf, g, tb, T * tb))
                    dve.sem_inc(passed, 1)

                start_block(0, 0)
                for tb in range(BLOCKS):
                    n, p = rows_of[tb], tb % 2

                    def next_input(gs, tau, parity):
                        for each in range(gs.start, gs.stop):
                            for j in range(2):
                                norm(p, 1 - parity, each, j, slice(0, n), tau + 1)

                    def step(tau, parity, ends_block=False):
                        for g in groups_in(tb):
                            gs, done = cells_in(tb, g), at(hf, g, T * tb) + tau
                            if tb < EARLY:
                                next_input(gs, tau, parity)
                            dve.wait_ge(gates_ready[g], done * 4 + 1)
                            v.tensor_tensor(fc[:, gs, 0:n], gate[:, gs, FORGET, 0:n], cell[:, gs, 0:n], ALU.mult)
                            dve.wait_ge(gates_ready[g], done * 4 + 3)
                            v.tensor_tensor(ig[:, gs, 0:n], gate[:, gs, IN, 0:n], gate[:, gs, CELL, 0:n], ALU.mult).then_inc(parts_ready[g], 1)
                            dve.wait_ge(parts_ready[g], done + 1)
                            v.tensor_tensor(cell[:, gs, 0:n], fc[:, gs, 0:n], ig[:, gs, 0:n], ALU.add).then_inc(cell_ready[g], 1)
                            if tb >= EARLY:
                                next_input(gs, tau, parity)
                            dve.wait_ge(gates_ready[g], done * 4 + 4)
                            dve.wait_ge(tanh_ready[g], done + 1)
                            for j in range(2):
                                ins = v.tensor_tensor(stack[hidden_at[j], 1 - parity, gs, j, 1:n + 1],
                                                      gate[pairs[j], gs, OUT, 0:n], tc[pairs[j], gs, 0:n], ALU.mult)
                            ins.then_inc(stack_ready[g], 1)
                            dve.wait_ge(added[g], done + 1)
                            v.tensor_tensor(hid[:, parity, gs, 0:n], gate[:, gs, OUT, 0:n], tc[:, gs, 0:n], ALU.mult).then_inc(hid_ready[g], 1)
                            if ends_block and tb + 1 < BLOCKS:
                                for each in (groups_in(tb + 1) if tb < EARLY else [g]):
                                    start_block(tb + 1, each)
                    steps(dve, hf, tb, step, 0, T - 2)
                    step(T - 2, 0)
                    step(T - 1, 1, ends_block=True)

        @block.gpsimd
        def _(pl):
            v = nc.gpsimd
            for g in range(GH):
                pl.sem_inc(added[g], 2)
            with pl.Fori(0, 2) as hf:
                for tb in range(BLOCKS):
                    n, p, rows = rows_of[tb], tb % 2, T * (tb + 1)
                    pl.wait_ge(ys_loaded[p], (hf * (BLOCKS // 2) + tb // 2 + 1) * 32)

                    def step(tau, parity):
                        for g in groups_in(tb):
                            gs, done = cells_in(tb, g), at(hf, g, T * tb) + tau
                            for each in range(gs.start, gs.stop):
                                if tb:
                                    cells = band[:, each, bass.ds(tau, 1), 0:T * tb].rearrange("p h t -> p (h t)")
                                    v.tensor_tensor(cells, cells, below[:, each, 0:T * tb], ALU.add)
                            pl.wait_ge(hid_ready[g], done + 2)
                            for each in range(gs.start, gs.stop):
                                if n < H:
                                    v.tensor_copy(below[:, each, bass.ds(T * tb + tau, 1)], hid[:, parity, each, n - 1:n])
                                cells = ys[p][:, each, 0:rows, bass.ds(tau, 1)].rearrange("p h t -> p (h t)")
                                ins = v.tensor_tensor(cells, cells, hid[:, parity, each, 0:rows], ALU.add)
                            ins.then_inc(added[g], 1)
                    for b in range(2):
                        if tb:
                            pl.wait_ge(band_loaded[b], (hf * (BLOCKS - 1) + tb) * 32)
                        steps(pl, hf, tb, step, T // 2 * b, T // 2 * (b + 1))
                    for g in groups_in(tb):
                        pl.wait_ge(added[g], at(hf, g, T * (tb + 1)) + 2)


def program(nc, x, const, out):
    x1 = nc.dram_tensor("x1", (NB, C, H, W), F32).ap()
    x3 = nc.dram_tensor("x3", (NB, C, H, WX), F32).ap()
    stats1 = nc.dram_tensor("stats1", (NB, C, 2), F32).ap()
    stats3 = nc.dram_tensor("stats3", (NB, C, 2), F32).ap()
    spectra = nc.dram_tensor("spectra", (NB, 2 * C, MM), F32).ap()
    mixed = nc.dram_tensor("mixed", (NB, 2 * C, MM), F32).ap()
    conv_phase(nc, 0, x["x"], x1, stats1, None, const, {"w": x["L0_conv_weight"]})
    spectrum_phase(nc, x1, spectra, const)
    mixing_phase(nc, spectra, stats1, x["L1_conv_weights1"], mixed)
    conv_phase(nc, 2, x1, x3, stats3, mixed, const,
               {"w1": x["L2_conv_w1"], "b1": x["L2_conv_b1"], "w2": x["L2_conv_w2"], "b2": x["L2_conv_b2"]})
    lstm_phase(nc, x3, out, stats3,
               {"W2": x["L3_conv_W2"], "W1": x["L3_conv_W1"], "b1": x["L3_conv_b1"], "b2": x["L3_conv_b2"]}, const)


def constants():
    import numpy as np
    p = np.arange(P)
    f = np.float64
    k = np.arange(M)
    ang_h = 2 * np.pi * np.outer(np.arange(H), k) / H
    ang_w = 2 * np.pi * np.outer(np.arange(W), k) / W
    i3 = np.zeros((P, 3, 2, C))
    for i in range(2):
        i3[C * (i + 1):C * (i + 2), 1, i, :] = np.eye(C)
    fh = np.concatenate([np.cos(ang_h), -np.sin(ang_h)], 1).reshape(2, P, 2 * M).transpose(1, 0, 2)
    fw = np.stack([np.concatenate([np.cos(ang_w), -np.sin(ang_w)], 1),
                   np.concatenate([np.sin(ang_w), np.cos(ang_w)], 1)], 1).reshape(2, P, 2, 2 * M).transpose(1, 0, 2, 3)
    eh = np.zeros((2 * C, H))
    eh[0:M] = np.cos(ang_h).T
    eh[C:C + M] = np.sin(ang_h).T
    twice = np.where(k == 0, 1.0, 2.0)[:, None] / (H * W)
    ew = np.concatenate([twice * np.cos(ang_w).T, -twice * np.sin(ang_w).T], 0)
    t = {
        "ident": np.eye(P),
        "g8": ((p[:, None] % C) // 2 == (p[None, :] % C) // 2) / 8.0,
        "g4": (p[:, None] % C == p[None, :] % C) / 4.0,
        "i3": i3.reshape(P, -1),
        "i4": (p[:, None] % C == np.arange(C)[None, :]) * 1.0,
        "ones": np.ones((P, PAD)),
        "fh": fh.reshape(P, -1), "fw": fw.reshape(P, -1), "eh": eh, "ew": ew,
    }
    return {n: np.ascontiguousarray(a, dtype=np.float32) for n, a in t.items()}


_INS = ['x', 'L0_conv_weight', 'L1_conv_weights1', 'L1_conv_weights2', 'L2_conv_w1', 'L2_conv_b1', 'L2_conv_w2',
        'L2_conv_b2', 'L3_conv_W2', 'L3_conv_b2', 'L3_conv_W1', 'L3_conv_b1']


def kernel(**inputs):
    import numpy as _np
    import concourse.bacc as _bacc
    from concourse import mybir as _mybir
    from concourse.bass_utils import run_bass_kernel_spmd as _run

    nc = _bacc.Bacc("TRN2", target_bir_lowering=False, num_devices=1)
    arrays, args, const = {}, {}, {}
    for name in _INS:
        a = _np.ascontiguousarray(inputs[name])
        arrays[f"in_{name}_dram"] = a
        args[name] = nc.dram_tensor(f"in_{name}_dram", a.shape, _mybir.dt.from_np(a.dtype), kind="ExternalInput").ap()
    for name, a in constants().items():
        arrays[f"const_{name}_dram"] = a
        const[name] = nc.dram_tensor(f"const_{name}_dram", a.shape, _mybir.dt.from_np(a.dtype), kind="ExternalInput").ap()
    out = nc.dram_tensor("out_0_dram", (NB, C, H, W), F32, kind="ExternalOutput").ap()
    program(nc, args, const, out)
    r = _run(nc, [arrays], core_ids=[0])
    return r.results[0]["out_0_dram"]
```
